# Optimizing a Trainium2 kernel written in Bass

```python
import numpy as np
import jax
import jax.numpy as jnp

def _softmax(x, axis=-1):
    return jax.nn.softmax(x, axis=axis)

def _gelu(x):
    return jax.nn.gelu(x, approximate=True)

def _silu(x):
    return jax.nn.silu(x)

def _sigmoid(x):
    return jax.nn.sigmoid(x)

def _layernorm(x, axis=-1, eps=1e-05):
    m = jnp.mean(x, axis=axis, keepdims=True)
    v = jnp.var(x, axis=axis, keepdims=True)
    return (x - m) / jnp.sqrt(v + eps)

def _scatter_add(tgt, idx, src, axis=0):
    return tgt.at[idx].add(src)

def _segment_sum(src, seg, n):
    return jax.ops.segment_sum(src, seg, n)
kernel_name = 'mk_prb_d1_jaxref_r8_2b4651'

def setup_inputs(seed: int=0):
    np.random.seed(seed)
    _w = jnp.asarray

    def _L0_attn_setup():
        import jax, jax.numpy as jnp
        import numpy as np
        B, N, D, H = (4, 512, 128, 16)
        HD = D // H

        def _kernel(x):
            return jax.nn.elu(x) + 1.0
        key = jax.random.key(seed)
        k1, k2, k3, k4 = jax.random.split(key, 4)
        x = jax.random.normal(k1, (B, N, D), dtype=jnp.float32)
        w_qkv = jax.random.normal(k2, (3 * D, D), dtype=jnp.float32) * (1.0 / np.sqrt(D))
        w_out = jax.random.normal(k3, (D, D), dtype=jnp.float32) * (1.0 / np.sqrt(D))
        b_out = jax.random.normal(k4, (D,), dtype=jnp.float32) * 0.01
        return {'x': x, 'w_qkv': w_qkv, 'w_out': w_out, 'b_out': b_out}
    _L0_attn_in = _L0_attn_setup()

    def _L0_ffn_setup():
        import jax, jax.numpy as jnp
        import numpy as np
        TOP_K = 2
        key = jax.random.key(seed)
        ks = jax.random.split(key, 5)
        B, S, H, I, E = (4, 256, 128, 512, 8)
        scale_hi = (2.0 / (H + I)) ** 0.5
        scale_he = (2.0 / (H + E)) ** 0.5
        return {'x': jax.random.normal(ks[0], (B, S, H), dtype=jnp.float32), 'router_w': jax.random.normal(ks[1], (E, H), dtype=jnp.float32) * scale_he, 'gate_w': jax.random.normal(ks[2], (E, I, H), dtype=jnp.float32) * scale_hi, 'up_w': jax.random.normal(ks[3], (E, I, H), dtype=jnp.float32) * scale_hi, 'down_w': jax.random.normal(ks[4], (E, H, I), dtype=jnp.float32) * scale_hi}
    _L0_ffn_in = _L0_ffn_setup()
    _d = {'L0_attn_x': _L0_attn_in['x'], 'L0_attn_w_qkv': _L0_attn_in['w_qkv'], 'L0_attn_w_out': _L0_attn_in['w_out'], 'L0_attn_b_out': _L0_attn_in['b_out'], 'L0_ffn_router_w': _L0_ffn_in['router_w'], 'L0_ffn_gate_w': _L0_ffn_in['gate_w'], 'L0_ffn_up_w': _L0_ffn_in['up_w'], 'L0_ffn_down_w': _L0_ffn_in['down_w']}
    _x0 = _d['L0_attn_x']
    _d['L0_attn_x'] = jax.random.normal(jax.random.fold_in(jax.random.key(seed), 1), (4, 512, 128), dtype=_x0.dtype)
    del _x0
    return _d

def reference(L0_attn_x, L0_attn_w_qkv, L0_attn_w_out, L0_attn_b_out, L0_ffn_router_w, L0_ffn_gate_w, L0_ffn_up_w, L0_ffn_down_w):

    def _L0_attn_ref(x, w_qkv, w_out, b_out):
        import jax, jax.numpy as jnp
        import numpy as np
        B, N, D, H = (4, 512, 128, 16)
        HD = D // H

        def _kernel(x):
            return jax.nn.elu(x) + 1.0
        b, n, d = x.shape
        qkv = x @ w_qkv.T
        qkv = qkv.reshape(b, n, 3, H, HD)
        q, k, v = (qkv[:, :, 0], qkv[:, :, 1], qkv[:, :, 2])
        q = _kernel(q)
        k = _kernel(k)
        kv = jnp.einsum('bnhd,bnhm->bhdm', k, v)
        z = 1.0 / (jnp.einsum('bnhd,bhd->bnh', q, k.sum(axis=1)) + 1e-06)
        out = jnp.einsum('bnhd,bhdm,bnh->bnhm', q, kv, z)
        out = out.reshape(b, n, d)
        return out @ w_out.T + b_out

    def _L0_ffn_ref(x, router_w, gate_w, up_w, down_w):
        import jax, jax.numpy as jnp
        import numpy as np
        TOP_K = 2
        B, S, H = x.shape
        E = router_w.shape[0]
        xf = x.reshape(-1, H)
        logits = xf @ router_w.T
        probs = jax.nn.softmax(logits, axis=-1)
        topk_p, topk_i = jax.lax.top_k(probs, TOP_K)
        topk_p = topk_p / topk_p.sum(axis=-1, keepdims=True)

        def body(out, inputs):
            e, gw, uw, dw = inputs
            sel = topk_i == e
            mask = sel.any(axis=-1)
            w_tok = (topk_p * sel).sum(axis=-1)
            cnt = mask.sum().astype(xf.dtype)
            mean_w = jnp.where(cnt > 0, w_tok.sum() / jnp.maximum(cnt, 1.0), 0.0)
            h = jax.nn.silu(xf @ gw.T) * (xf @ uw.T)
            eo = h @ dw.T
            out = out + mask[:, None].astype(xf.dtype) * eo * mean_w
            return (out, None)
        out0 = jnp.zeros_like(xf)
        out, _ = jax.lax.scan(body, out0, (jnp.arange(E), gate_w, up_w, down_w))
        return out.reshape(B, S, H)
    x = L0_attn_x
    xn = _layernorm(x, axis=-1)
    x = x + _L0_attn_ref(xn, L0_attn_w_qkv, L0_attn_w_out, L0_attn_b_out) + _L0_ffn_ref(xn, L0_ffn_router_w, L0_ffn_gate_w, L0_ffn_up_w, L0_ffn_down_w)
    return x

_drawn_inputs = setup_inputs


def setup_inputs(seed=0):
    import zlib

    import numpy as np

    out = dict(_drawn_inputs(seed))
    spreads = {}
    factors = {'L0_attn_b_out': 5.642}
    for name, (base, spread) in spreads.items():
        noise = np.random.default_rng([zlib.crc32(name.encode()), seed]).standard_normal(out[name].shape)
        drawn = base * np.exp(spread * noise) if base else spread * noise
        out[name] = jnp.asarray(drawn.astype(out[name].dtype))
    for name, factor in factors.items():
        out[name] = (out[name] * factor).astype(out[name].dtype)
    return out
```

```python
from contextlib import ExitStack

import numpy as np
import concourse.bass as bass
from concourse import mybir

F32 = mybir.dt.float32
F16 = mybir.dt.float16
I32 = mybir.dt.int32
U32 = mybir.dt.uint32
ALU = mybir.AluOpType
ACT = mybir.ActivationFunctionType
AX_X = mybir.AxisListType.X

P = 128
D = 128
NBATCH, SEQ = 4, 512
T = NBATCH * SEQ
NT = T // P
TPB = SEQ // P
H, HD = 16, 8
E, I = 8, 512
IC = I // P
TOP = 2
NS = (TOP * T + E * (P - 1)) // P
RING = 3
NR = NS // RING
assert NR * RING == NS
NW = D + H
LN_EPS, Z_EPS = 1e-5, 1e-6
NO_ROW = 2 * TOP * T

_SIZES = dict(ident=P, upper=P, ones=P, prefix=P, total=E, rev=E, tiles=NS, lanes=P, steps=NT,
              below=E * E, code=TOP * NT, heads=D, headsel=H)
COL, _at = {}, 0
for _name, _n in _SIZES.items():
    COL[_name] = (_at, _at + _n)
    _at += _n
NCONST = _at


def constants():
    c = np.zeros((P, NCONST), np.float32)
    p = np.arange(P)

    def put(name, value):
        c[:, COL[name][0]:COL[name][1]] = value

    put("ident", np.eye(P))
    put("upper", p[:, None] < p[None, :])
    put("ones", 1.0)
    tile, expert = p // E, p % E
    put("prefix", (expert[:, None] == expert) & (tile[:, None] < tile))
    put("total", expert[:, None] == np.arange(E))
    put("rev", E - np.arange(E))
    put("tiles", np.arange(NS))
    put("lanes", p)
    put("steps", P * np.arange(NT))
    put("below", (np.arange(E)[None, :] < np.arange(E)[:, None]).reshape(-1))
    token = P * np.arange(NT)[None, :] + p[:, None] + 1
    put("code", np.concatenate([-token, token], 1))
    put("heads", (p[:, None] // HD) == (p[None, :] // HD))
    put("headsel", (p[:, None] // HD) == np.arange(H))
    return c


def moe_attention_block(nc, x, wqkv, wout, bout, router, gate, up, down, const, out):
    with ExitStack() as ctx:
        def sb(name, shape, dt=F32):
            return ctx.enter_context(nc.sbuf_tensor(name, shape, dt))

        def sem(name):
            return ctx.enter_context(nc.semaphore(name))

        bank = [ctx.enter_context(nc.psum_tensor(f"bank{n}", [P, 512], F32)) for n in range(8)]
        xn_rows = nc.dram_tensor("xn_rows", (T, D), F32, kind="Internal").ap()
        expert_rows = nc.dram_tensor("expert_rows", (TOP * T, D), F32, kind="Internal").ap()

        X = sb("X", [P, NT, D])
        XN = sb("XN", [P, NT, D])
        XNT = sb("XNT", [P, T])
        Wqkv = sb("Wqkv", [P, 3 * D])
        Wout = sb("Wout", [P, D])
        Bout = sb("Bout", [P, D])
        Wr = sb("Wr", [P, E])
        Wg = sb("Wg", [P, E * I])
        Wu = sb("Wu", [P, E * I])
        Wd = sb("Wd", [P, E * I])
        K = sb("K", [P, NCONST])
        stats = sb("stats", [P, NT, 6])
        mv = sb("mv", [P, NT, 2])
        var = sb("var", [P, NT])
        std = sb("std", [P, NT])
        rstd = sb("rstd", [P, NT])
        newt = sb("newt", [P, NT])
        rs = sb("rs", [P, NT])
        ek = sb("ek", [P, 2, SEQ])
        rk = sb("rk", [P, 2, SEQ])
        eq = sb("eq", [P, 2, SEQ])
        rq = sb("rq", [P, 2, SEQ])
        PK = sb("PK", [P, NBATCH, SEQ])
        PQ = sb("PQ", [P, NBATCH, SEQ])
        V1 = sb("V1", [P, NT, D + 1])
        KVR = sb("KVR", [P, NBATCH, NW])
        den = sb("den", [P, 2, H])
        z = sb("z", [P, 2, H])
        O = sb("O", [P, NT, D])
        OT = sb("OT", [P, 2, SEQ])
        XB = sb("XB", [P, NT, D])
        top1 = sb("top1", [P, NT])
        Ls = sb("Ls", [P, NT, E])
        Ex = sb("Ex", [P, NT, E])
        ssum = sb("ssum", [P, NT])
        rsum = sb("rsum", [P, NT])
        Pr = sb("Pr", [P, NT, E])
        Pr2 = sb("Pr2", [P, NT, E])
        pk = sb("pk", [P, TOP, NT])
        cand = sb("cand", [P, NT, E])
        rk1 = sb("rk1", [P, NT])
        OH = sb("OH", [P, TOP, NT, E])
        M16 = sb("M16", [P, NT * E], F16)
        psum2 = sb("psum2", [P, NT])
        rp2 = sb("rp2", [P, NT])
        wk = sb("wk", [P, TOP, NT])
        WT = sb("WT", [P, TOP, NT, E])
        WTs = sb("WTs", [P, NT, E])
        upper16 = sb("upper16", [P, P], F16)
        ones16 = sb("ones16", [P, P], F16)
        prefix16 = sb("prefix16", [P, P], F16)
        total16 = sb("total16", [P, E], F16)
        lanes16 = sb("lanes16", [P, P], F16)
        tot16 = sb("tot16", [P, P], F16)
        cnt = sb("cnt", [P, E])
        gt = sb("gt", [P, E, NT])
        ntile = sb("ntile", [P, E])
        basep = sb("basep", [P, E, E])
        base = sb("base", [P, E])
        slot = sb("slot", [P, NT, E])
        pos = sb("pos", [P, TOP, NT])
        posi = sb("posi", [P, TOP * NT], I32)
        hi = sb("hi", [P, TOP * NT], I32)
        lo = sb("lo", [P, TOP * NT], I32)
        lof = sb("lof", [P, TOP * NT])
        hif = sb("hif", [P, TOP * NT])
        OHcode = sb("OHcode", [P, TOP * NT, NS], F16)
        OHlo = sb("OHlo", [P, TOP * NT, P], F16)
        code = sb("code_of_slot", [P, NS])
        row1 = sb("row1", [P, NS])
        second = sb("second", [P, NS])
        pad = sb("pad", [P, NS])
        IDX = sb("IDX", [P, NS, 2], U32)
        ge = sb("ge", [P, NS, E])
        eid = sb("eid", [P, NS + 1])
        words = sb("words", [P, NR])
        word = sb("word", [P, NR], I32)
        sumw = sb("sumw", [P, E])
        meanw = sb("meanw", [P, E])
        scale = sb("scale", [P, NS])
        gidx = sb("gidx", [P, RING, 1], U32)
        sidx = sb("sidx", [P, RING, 1], U32)
        XG = sb("XG", [P, RING, D])
        XGT = sb("XGT", [P, RING, P])
        SG = sb("SG", [P, I])
        HG = sb("HG", [P, I])
        HT = sb("HT", [P, I])
        Y = sb("Y", [P, RING, D])
        Y01 = sb("Y01", [P, TOP, NT, D])

        def k_(name, n=None):
            a, b = COL[name]
            return K[:, a:b]

        def over_tiles(ap, n=NT):
            return ap.unsqueeze(1).to_broadcast([P, n, E])

        def over_experts(ap, n=NT):
            return ap.unsqueeze(2).to_broadcast([P, n, E])

        x_loaded = [sem(f"x_loaded{q}") for q in range(NBATCH)]
        const_loaded = sem("const_loaded")
        attn_weights_loaded = sem("attn_weights_loaded")
        gate_loaded = sem("gate_loaded")
        up_loaded = sem("up_loaded")
        down_loaded = sem("down_loaded")
        dve_step = sem("dve_step")
        var_ready = sem("var_ready")
        std_ready = sem("std_ready")
        xn_ready = sem("xn_ready")
        xn_stored = sem("xn_stored")
        xt_made = sem("xt_made")
        xt_copied = sem("xt_copied")
        consts16 = sem("consts16")
        logits_made = sem("logits_made")
        shifted = sem("shifted")
        exp_ready = sem("exp_ready")
        chosen = sem("chosen")
        tot_made = sem("tot_made")
        tot_copied = sem("tot_copied")
        rank_made = sem("rank_made")
        weights_ready = sem("weights_ready")
        sumw_made = sem("sumw_made")
        lanes_split = sem("lanes_split")
        lo_ready = sem("lo_ready")
        hi_ready = sem("hi_ready")
        pool_step = sem("pool_step")
        code_made = sem("code_made")
        index_ready = sem("index_ready")
        word_ready = sem("word_ready")
        k_made = sem("k_made")
        v_made = sem("v_made")
        q_made = sem("q_made")
        k_taken = sem("k_taken")
        v_taken = sem("v_taken")
        q_taken = sem("q_taken")
        phik_ready = sem("phik_ready")
        phiq_ready = sem("phiq_ready")
        v_ones = sem("v_ones")
        kv_made = sem("kv_made")
        kv_ready = sem("kv_ready")
        num_made = sem("num_made")
        o_ready = sem("o_ready")
        ot_made = sem("ot_made")
        ot_copied = sem("ot_copied")
        proj_made = sem("proj_made")
        proj_added = sem("proj_added")
        xb_ready = sem("xb_ready")
        gathered = [sem(f"gathered{r}") for r in range(RING)]
        scattered = [sem(f"scattered{r}") for r in range(RING)]
        indices_copied = sem("indices_copied")
        xgt_made = sem("xgt_made")
        xgt_copied = sem("xgt_copied")
        gate_made = sem("gate_made")
        up_made = sem("up_made")
        silu_ready = sem("silu_ready")
        hidden_ready = sem("hidden_ready")
        ht_made = sem("ht_made")
        ht_copied = sem("ht_copied")
        y_made = sem("y_made")
        y_ready = sem("y_ready")
        first_loaded = [sem(f"first_loaded{q}") for q in range(NBATCH)]
        second_loaded = [sem(f"second_loaded{q}") for q in range(NBATCH)]
        final_step = sem("final_step")
        final_ready = sem("final_ready")
        out_stored = sem("out_stored")

        x_d = x.rearrange("(q c p) d -> q p c d", p=P, c=TPB)
        xn_d = xn_rows.rearrange("(q c p) d -> q p c d", p=P, c=TPB)
        er_d = expert_rows.rearrange("(k q c p) d -> k q p c d", k=TOP, p=P, c=TPB)
        out_d = out.rearrange("(q c p) d -> q p c d", p=P, c=TPB)

        def quarter(buf, q):
            return buf[:, q * TPB:(q + 1) * TPB, :]

        block = ctx.enter_context(nc.Block())

        @block.sync
        def _(sp):
            for q in range(NBATCH):
                sp.dma_start(quarter(X, q), x_d[q]).then_inc(x_loaded[q], 16)
            sp.dma_start(Wr[:], router).then_inc(attn_weights_loaded, 16)
            sp.dma_start(Wqkv[:], wqkv).then_inc(attn_weights_loaded, 16)
            sp.dma_start(Wout[:], wout).then_inc(attn_weights_loaded, 16)
            sp.dma_start(Bout[:], bout.partition_broadcast(P)).then_inc(attn_weights_loaded, 16)
            sp.dma_start(Wg[:], gate).then_inc(gate_loaded, 16)
            sp.dma_start(Wu[:], up).then_inc(up_loaded, 16)
            sp.dma_start(Wd[:], down).then_inc(down_loaded, 16)
            for r in range(RING):
                sp.wait_ge(scattered[r], 16 * NR)
            for q in range(NBATCH):
                sp.dma_start(quarter(Y01[:, 0], q), er_d[0, q]).then_inc(first_loaded[q], 16)
            for q in range(NBATCH):
                sp.wait_ge(final_ready, q + 1)
                sp.dma_start(out_d[q], quarter(X, q)).then_inc(out_stored, 16)
            sp.wait_ge(out_stored, 16 * NBATCH)

        @block.scalar
        def _(act):
            act.dma_start(K[:], const).then_inc(const_loaded, 16)
            act.wait_ge(var_ready, 1)
            nc.scalar.activation(std[:], var[:], ACT.Sqrt).then_inc(std_ready, 1)
            for q in range(NBATCH):
                act.wait_ge(xt_made, q + 1)
                nc.scalar.copy(XNT[:, q * SEQ:(q + 1) * SEQ], bank[q % 2][:]).then_inc(xt_copied, 1)
                act.wait_ge(xn_ready, (q + 1) * TPB)
                act.dma_start(xn_d[q], quarter(XN, q)).then_inc(xn_stored, 16)
            act.wait_ge(shifted, 1)
            nc.scalar.activation(Ex[:], Ls[:], ACT.Exp).then_inc(exp_ready, 1)
            for b in range(NBATCH):
                if b >= 2:
                    act.wait_ge(phik_ready, b - 1)
                act.wait_ge(k_made, b + 1)
                nc.scalar.activation(ek[:, b % 2], bank[0][:], ACT.Exp)
                nc.scalar.activation(rk[:, b % 2], bank[0][:], ACT.Relu).then_inc(k_taken, 1)
                act.wait_ge(v_made, b + 1)
                nc.scalar.copy(V1[:, b * TPB:(b + 1) * TPB, 0:D],
                               bank[1][:].rearrange("p (c d) -> p c d", d=D)).then_inc(v_taken, 1)
                if b >= 2:
                    act.wait_ge(phiq_ready, b - 1)
                act.wait_ge(q_made, b + 1)
                nc.scalar.activation(eq[:, b % 2], bank[2][:], ACT.Exp)
                nc.scalar.activation(rq[:, b % 2], bank[2][:], ACT.Relu).then_inc(q_taken, 1)
            for b in range(NBATCH):
                act.wait_ge(ot_made, b + 1)
                if b >= 2:
                    act.wait_ge(proj_made, b - 1)
                nc.scalar.copy(OT[:, b % 2], bank[2][:]).then_inc(ot_copied, 1)

            def activate(s, first=False):
                act.wait_ge(gate_made, s + 1)
                if not first:
                    act.wait_ge(hidden_ready, s)
                nc.scalar.activation(SG[:], bank[0][:], ACT.Silu).then_inc(silu_ready, 1)
                act.wait_ge(ht_made, s + 1)
                if not first:
                    act.wait_ge(y_made, s)
                nc.scalar.copy(HT[:], bank[2][:]).then_inc(ht_copied, 1)

            activate(0, first=True)
            with act.Fori(1, NS) as s:
                activate(s)

            for q in range(NBATCH):
                if q == 0:
                    for r in range(RING):
                        act.wait_ge(scattered[r], 16 * NR)
                act.dma_start(quarter(Y01[:, 1], q), er_d[1, q]).then_inc(second_loaded[q], 16)

        @block.gpsimd
        def _(pool):
            steps = [0]

            def step(ins):
                steps[0] += 1
                ins.then_inc(pool_step, 1)
                pool.wait_ge(pool_step, steps[0])

            nc.gpsimd.memset(V1[:, :, D:D + 1], 1.0).then_inc(v_ones, 1)
            pool.wait_ge(const_loaded, 16)
            nc.gpsimd.tensor_copy(upper16[:], k_("upper"))
            nc.gpsimd.tensor_copy(ones16[:], k_("ones"))
            nc.gpsimd.tensor_copy(prefix16[:], k_("prefix"))
            nc.gpsimd.tensor_copy(total16[:], k_("total"))
            nc.gpsimd.tensor_copy(lanes16[:], k_("lanes")).then_inc(consts16, 1)
            pool.wait_ge(consts16, 1)
            for q in range(NBATCH):
                pool.wait_ge(x_loaded[q], 16)
            pool.wait_ge(attn_weights_loaded, 64)
            nc.gpsimd.tensor_tensor(XB[:], X[:], Bout[:].unsqueeze(1).to_broadcast([P, NT, D]),
                                    ALU.add).then_inc(xb_ready, 1)

            def phi(b):
                for taken, ez, pz, to, done in ((k_taken, ek, rk, PK, phik_ready),
                                                (q_taken, eq, rq, PQ, phiq_ready)):
                    pool.wait_ge(taken, b + 1)
                    step(nc.gpsimd.tensor_scalar(ez[:, b % 2], ez[:, b % 2], 1.0, None, ALU.min))
                    nc.gpsimd.tensor_tensor(to[:, b], ez[:, b % 2], pz[:, b % 2], ALU.add).then_inc(done, 1)

            phi(0)
            phi(1)
            phi(2)
            pool.wait_ge(lanes_split, 1)
            for c in range(TOP * NT):
                nc.gpsimd.tensor_scalar(OHcode[:, c], k_("tiles"), hif[:, c:c + 1], k_("code")[:, c:c + 1],
                                        ALU.is_equal, ALU.mult).then_inc(hi_ready, 1)
            phi(3)

            pool.wait_ge(index_ready, 1)
            pool.wait_ge(xn_stored, 16 * NBATCH)

            def gather(r, tile):
                nc.gpsimd.tensor_copy(gidx[:, r], IDX[:, tile, 0:1]).then_inc(indices_copied, 1)
                pool.wait_ge(indices_copied, 1)
                nc.gpsimd.indirect_dma_start(
                    XG[:, r], None, xn_rows, bass.IndirectOffsetOnAxis(gidx[:, r], 0)).then_inc(gathered[r], 16)
                pool.sem_clear(indices_copied)

            def scatter(r, tile):
                nc.gpsimd.tensor_copy(sidx[:, r], IDX[:, tile, 1:2]).then_inc(indices_copied, 1)
                pool.wait_ge(indices_copied, 1)
                nc.gpsimd.indirect_dma_start(
                    expert_rows, bass.IndirectOffsetOnAxis(sidx[:, r], 0), Y[:, r], None,
                    bounds_check=TOP * T - 1, oob_is_err=False).then_inc(scattered[r], 16)
                pool.sem_clear(indices_copied)

            for r in range(RING):
                gather(r, slice(r, r + 1))
            with pool.Fori(0, NR - 1) as i:
                for r in range(RING):
                    s = i * RING + r
                    pool.wait_ge(xgt_made, s + 1)
                    gather(r, bass.ds(s + RING, 1))
                    pool.wait_ge(y_ready, s + 1)
                    scatter(r, bass.ds(s, 1))
            for r in range(RING):
                s = NS - RING + r
                pool.wait_ge(y_ready, s + 1)
                scatter(r, slice(s, s + 1))
            for r in range(RING):
                pool.wait_ge(scattered[r], 16 * NR)

        @block.vector
        def _(dve):
            steps = [0]

            def step(ins):
                steps[0] += 1
                ins.then_inc(dve_step, 1)
                dve.wait_ge(dve_step, steps[0])

            v = nc.vector
            for q in range(NBATCH):
                dve.wait_ge(x_loaded[q], 16)
                for t in range(q * TPB, (q + 1) * TPB):
                    last = v.bn_stats(stats[:, t], X[:, t])
            step(last)
            for t in range(NT):
                last = v.bn_aggr(mv[:, t], stats[:, t])
            step(last)
            v.tensor_scalar(var[:], mv[:, :, 1], LN_EPS, None, ALU.add).then_inc(var_ready, 1)
            dve.wait_ge(std_ready, 1)
            step(v.reciprocal(rstd[:], std[:]))
            step(v.tensor_tensor(newt[:], rstd[:], rstd[:], ALU.mult))
            step(v.tensor_tensor(newt[:], newt[:], var[:], ALU.mult))
            step(v.tensor_scalar(newt[:], newt[:], -0.5, 1.5, ALU.mult, ALU.add))
            step(v.tensor_tensor(rs[:], rstd[:], newt[:], ALU.mult))
            for t in range(NT):
                v.tensor_scalar(XN[:, t], X[:, t], mv[:, t, 0:1], rs[:, t:t + 1],
                                ALU.subtract, ALU.mult).then_inc(xn_ready, 1)

            dve.wait_ge(const_loaded, 16)
            dve.wait_ge(logits_made, 1)
            L = bank[3][:, 0:NT * E].rearrange("p (t e) -> p t e", e=E)
            step(v.tensor_reduce(top1[:], L, AX_X, ALU.max))
            v.tensor_tensor(Ls[:], L, over_experts(top1[:]), ALU.subtract).then_inc(shifted, 1)
            dve.wait_ge(exp_ready, 1)
            step(v.tensor_reduce(ssum[:], Ex[:], AX_X, ALU.add))
            step(v.reciprocal(rsum[:], ssum[:]))
            step(v.tensor_tensor(Pr[:], Ex[:], over_experts(rsum[:]), ALU.mult))

            def choose(k, prob):
                step(v.tensor_reduce(pk[:, k], prob[:], AX_X, ALU.max))
                step(v.tensor_tensor(cand[:], prob[:], over_experts(pk[:, k]), ALU.is_ge))
                step(v.tensor_tensor(cand[:], cand[:], over_tiles(k_("rev")), ALU.mult))
                step(v.tensor_reduce(rk1[:], cand[:], AX_X, ALU.max))
                step(v.tensor_tensor(OH[:, k], over_tiles(k_("rev")), over_experts(rk1[:]), ALU.is_equal))

            choose(0, Pr)
            step(v.scalar_tensor_tensor(Pr2[:], OH[:, 0], -2.0, Pr[:], ALU.mult, ALU.add))
            choose(1, Pr2)
            v.tensor_tensor(M16[:].rearrange("p (t e) -> p t e", e=E), OH[:, 0], OH[:, 1],
                            ALU.add).then_inc(chosen, 1)

            step(v.tensor_tensor(psum2[:], pk[:, 0], pk[:, 1], ALU.add))
            step(v.reciprocal(rp2[:], psum2[:]))
            for k in range(TOP):
                last = v.tensor_tensor(wk[:, k], pk[:, k], rp2[:], ALU.mult)
            step(last)
            dve.wait_ge(tot_made, 1)
            v.tensor_copy(tot16[:], bank[3][:, 256:384]).then_inc(tot_copied, 1)
            for k in range(TOP):
                last = v.tensor_tensor(WT[:, k], OH[:, k], over_experts(wk[:, k]), ALU.mult)
            step(last)
            v.tensor_tensor(WTs[:], WT[:, 0], WT[:, 1], ALU.add).then_inc(weights_ready, 1)

            dve.wait_ge(rank_made, 1)
            step(v.tensor_copy(cnt[:], bank[4][:, P:P + E]))
            step(v.tensor_tensor(gt[:], cnt[:].unsqueeze(2).to_broadcast([P, E, NT]),
                                 k_("steps").unsqueeze(1).to_broadcast([P, E, NT]), ALU.is_gt))
            step(v.tensor_reduce(ntile[:], gt[:], AX_X, ALU.add))
            step(v.tensor_tensor(basep[:], ntile[:].unsqueeze(1).to_broadcast([P, E, E]),
                                 k_("below").rearrange("p (a b) -> p a b", b=E), ALU.mult))
            step(v.tensor_reduce(base[:], basep[:], AX_X, ALU.add))
            step(v.scalar_tensor_tensor(slot[:], over_tiles(base[:]), float(P),
                                        bank[4][:, 0:P].rearrange("p (t e) -> p t e", e=E),
                                        ALU.mult, ALU.add))
            for k in range(TOP):
                step(v.tensor_tensor(cand[:], OH[:, k], slot[:], ALU.mult))
                step(v.tensor_reduce(pos[:, k], cand[:], AX_X, ALU.add))
            step(v.tensor_copy(posi[:], pos[:].rearrange("p k t -> p (k t)")))
            v.tensor_scalar(hi[:], posi[:], 7, None, ALU.arith_shift_right)
            step(v.tensor_scalar(lo[:], posi[:], P - 1, None, ALU.bitwise_and))
            v.tensor_copy(lof[:], lo[:])
            v.tensor_copy(hif[:], hi[:]).then_inc(lanes_split, 1)
            dve.wait_ge(lanes_split, 1)
            dve.wait_ge(consts16, 1)
            for c in range(TOP * NT):
                v.tensor_scalar(OHlo[:, c], lanes16[:], lof[:, c:c + 1], None,
                                ALU.is_equal).then_inc(lo_ready, 1)

            step(v.tensor_tensor(ge[:], k_("tiles").unsqueeze(2).to_broadcast([P, NS, E]),
                                 over_tiles(base[:], NS), ALU.is_ge))
            step(v.tensor_reduce(eid[:, 0:NS], ge[:], AX_X, ALU.add))
            step(v.tensor_scalar(eid[:, 0:NS], eid[:, 0:NS], -1.0, None, ALU.add))
            step(v.tensor_copy(eid[:, NS:NS + 1], eid[:, NS - 1:NS]))
            def nth(n):
                return eid[:, n:n + (NR - 1) * RING + 1:RING]
            step(v.scalar_tensor_tensor(words[:], nth(3), float(E), nth(2), ALU.mult, ALU.add))
            step(v.scalar_tensor_tensor(words[:], words[:], float(E), nth(1), ALU.mult, ALU.add))
            step(v.scalar_tensor_tensor(words[:], words[:], float(E), nth(0), ALU.mult, ALU.add))
            v.tensor_copy(word[:], words[:]).then_inc(word_ready, 1)

            dve.wait_ge(code_made, 1)
            step(v.tensor_copy(code[:], bank[3][:, P:P + NS]))
            step(v.scalar_tensor_tensor(row1[:], code[:], -1.0, code[:], ALU.mult, ALU.max))
            v.tensor_scalar(IDX[:, :, 0], row1[:], -1.0, 0.0, ALU.add, ALU.max)
            v.tensor_scalar(second[:], code[:], 0.0, float(T), ALU.is_gt, ALU.mult)
            step(v.tensor_scalar(pad[:], code[:], 0.0, float(NO_ROW), ALU.is_equal, ALU.mult))
            step(v.scalar_tensor_tensor(row1[:], row1[:], -1.0, second[:], ALU.add, ALU.add))
            v.tensor_tensor(IDX[:, :, 1], row1[:], pad[:], ALU.add).then_inc(index_ready, 1)

            dve.wait_ge(sumw_made, 1)
            step(v.tensor_reduce(sumw[:], bank[7][:, 0:NT * E].rearrange("p (t e) -> p e t", e=E),
                                 AX_X, ALU.add))
            step(v.tensor_scalar(cnt[:], cnt[:], 1.0, None, ALU.max))
            step(v.reciprocal(cnt[:], cnt[:]))
            step(v.tensor_tensor(meanw[:], sumw[:], cnt[:], ALU.mult))
            step(v.tensor_scalar(eid[:, 0:NS], eid[:, 0:NS], -1.0, float(E), ALU.mult, ALU.add))
            step(v.tensor_tensor(ge[:], over_tiles(k_("rev"), NS), over_experts(eid[:, 0:NS], NS),
                                 ALU.is_equal))
            step(v.tensor_tensor(ge[:], ge[:], over_tiles(meanw[:], NS), ALU.mult))
            step(v.tensor_reduce(scale[:], ge[:], AX_X, ALU.add))

            for b in range(NBATCH):
                dve.wait_ge(kv_made, NBATCH)
                kv = bank[5][:, b * (D + 1):(b + 1) * (D + 1)] if b < 3 else bank[6][:, 0:D + 1]
                v.tensor_tensor(KVR[:, b, 0:D], kv[:, 0:D], k_("heads"), ALU.mult)
                v.tensor_tensor(KVR[:, b, D:NW], kv[:, D:D + 1].to_broadcast([P, H]), k_("headsel"),
                                ALU.mult).then_inc(kv_ready, 1)
            dve.wait_ge(xb_ready, 1)

            def add_projection(b):
                dve.wait_ge(proj_made, b + 1)
                v.tensor_tensor(quarter(X, b), quarter(XB, b),
                                bank[b % 2][:].rearrange("p (c d) -> p c d", d=D),
                                ALU.add).then_inc(proj_added, 1)

            for j in range(NT // 2):
                dve.wait_ge(num_made, j + 1)
                nd = bank[6 + j % 2][:, 0:2 * NW].rearrange("p (c n) -> p c n", n=NW)
                step(v.tensor_scalar(den[:], nd[:, :, D:NW], Z_EPS, None, ALU.add))
                step(v.reciprocal(z[:], den[:]))
                v.tensor_tensor(O[:, 2 * j:2 * j + 2].rearrange("p c (h d) -> p c h d", d=HD),
                                nd[:, :, 0:D].rearrange("p c (h d) -> p c h d", d=HD),
                                z[:].unsqueeze(3).to_broadcast([P, 2, H, HD]),
                                ALU.mult).then_inc(o_ready, 1)
                if j % 2 == 1 and j >= 3:
                    add_projection(j // 2 - 1)
            add_projection(NBATCH - 1)

            def rows_copied(n, s):
                dve.wait_ge(xgt_made, s + 1)
                v.tensor_copy(XGT[:, n], bank[3][:, 0:P]).then_inc(xgt_copied, 1)

            def hidden(s, first):
                dve.wait_ge(silu_ready, s + 1)
                dve.wait_ge(up_made, s + 1)
                if not first:
                    dve.wait_ge(ht_made, s)
                v.tensor_tensor(HG[:], SG[:], bank[1][:], ALU.mult).then_inc(hidden_ready, 1)

            def result(r, s, turn, tile):
                dve.wait_ge(y_made, s + 1)
                if turn is not None:
                    dve.wait_ge(scattered[r], turn * 16)
                v.tensor_scalar(Y[:, r], bank[4][:, 0:D], scale[:, tile], None,
                                ALU.mult).then_inc(y_ready, 1)

            def turn(i, first=False, last=False):
                for r in range(RING):
                    s = i * RING + r
                    hidden(s, first and r == 0)
                    if not last or r + 2 < RING:
                        rows_copied((r + 2) % RING, s + 2)
                    result(r, s, None if first else i,
                           slice(s, s + 1) if first or last else bass.ds(s, 1))

            rows_copied(0, 0)
            rows_copied(1, 1)
            turn(0, first=True)
            with dve.Fori(1, NR - 1) as i:
                turn(i)
            turn(NR - 1, last=True)

            for q in range(NBATCH):
                dve.wait_ge(first_loaded[q], 16)
                v.tensor_tensor(quarter(X, q), quarter(X, q), quarter(Y01[:, 0], q),
                                ALU.add).then_inc(final_step, 1)
                dve.wait_ge(final_step, q + 1)
                dve.wait_ge(second_loaded[q], 16)
                v.tensor_tensor(quarter(X, q), quarter(X, q), quarter(Y01[:, 1], q),
                                ALU.add).then_inc(final_ready, 1)

        @block.tensor
        def _(pe):
            mm, tp = nc.tensor.matmul, nc.tensor.transpose
            ident = k_("ident")
            pe.wait_ge(const_loaded, 16)
            for q in range(NBATCH):
                if q >= 2:
                    pe.wait_ge(xt_copied, q - 1)
                for c in range(TPB):
                    t = q * TPB + c
                    pe.wait_ge(xn_ready, t + 1)
                    last = tp(bank[q % 2][:, c * P:(c + 1) * P], XN[:, t], ident)
                last.then_inc(xt_made, 1)
            pe.wait_ge(attn_weights_loaded, 64)
            for t in range(NT):
                if t % TPB == 0:
                    pe.wait_ge(xt_copied, t // TPB + 1)
                last = mm(bank[3][:, t * E:(t + 1) * E], XNT[:, t * P:(t + 1) * P], Wr[:],
                          start=True, stop=True)
            last.then_inc(logits_made, 1)

            def kv_sum(b):
                pe.wait_ge(phik_ready, b + 1)
                pe.wait_ge(v_taken, b + 1)
                o = bank[5][:, b * (D + 1):(b + 1) * (D + 1)] if b < 3 else bank[6][:, 0:D + 1]
                for c in range(TPB):
                    last = mm(o, PK[:, b, c * P:(c + 1) * P], V1[:, b * TPB + c],
                              start=(c == 0), stop=(c == TPB - 1))
                last.then_inc(kv_made, 1)

            def project_in(b):
                for n, taken, made in ((1, k_taken, k_made), (2, v_taken, v_made)):
                    if b:
                        pe.wait_ge(taken, b)
                    for c in range(TPB):
                        t = b * TPB + c
                        last = mm(bank[n - 1][:, c * P:(c + 1) * P], XNT[:, t * P:(t + 1) * P],
                                  Wqkv[:, n * D:(n + 1) * D], start=True, stop=True)
                    last.then_inc(made, 1)
                if b:
                    pe.wait_ge(q_taken, b)
                mm(bank[2][:], Wqkv[:, 0:D], XNT[:, b * SEQ:(b + 1) * SEQ],
                   start=True, stop=True).then_inc(q_made, 1)

            project_in(0)
            project_in(1)
            kv_sum(0)
            pe.wait_ge(chosen, 1)
            pe.wait_ge(consts16, 1)
            mm(bank[3][:, 256:384], M16[:], ones16[:], start=True, stop=True).then_inc(tot_made, 1)
            mm(bank[4][:, 0:P], upper16[:], M16[:], start=True, stop=False)
            pe.wait_ge(tot_copied, 1)
            mm(bank[4][:, 0:P], tot16[:], prefix16[:], start=False, stop=True)
            mm(bank[4][:, P:P + E], tot16[:], total16[:], start=True, stop=True).then_inc(rank_made, 1)
            project_in(2)
            kv_sum(1)
            pe.wait_ge(weights_ready, 1)
            mm(bank[7][:, 0:NT * E], k_("ones"), WTs[:].rearrange("p t e -> p (t e)"),
               start=True, stop=True).then_inc(sumw_made, 1)
            project_in(3)
            kv_sum(2)
            for c in range(TOP * NT):
                pe.wait_ge(lo_ready, c + 1)
                pe.wait_ge(hi_ready, c + 1)
                last = mm(bank[3][:, P:P + NS], OHlo[:, c], OHcode[:, c],
                          start=(c == 0), stop=(c == TOP * NT - 1))
            last.then_inc(code_made, 1)
            kv_sum(3)

            def numerators(j):
                if j == 0:
                    pe.wait_ge(kv_ready, NBATCH)
                if j >= 2:
                    pe.wait_ge(o_ready, j - 1)
                for c in range(2):
                    t = 2 * j + c
                    b = t // TPB
                    last = mm(bank[6 + j % 2][:, c * NW:(c + 1) * NW],
                              PQ[:, b, (t % TPB) * P:(t % TPB + 1) * P], KVR[:, b],
                              start=True, stop=True)
                last.then_inc(num_made, 1)

            def turn_out(b):
                pe.wait_ge(o_ready, 2 * b + 2)
                if b:
                    pe.wait_ge(ot_copied, b)
                for c in range(TPB):
                    last = tp(bank[2][:, c * P:(c + 1) * P], O[:, b * TPB + c], ident)
                last.then_inc(ot_made, 1)

            def project_out(b):
                pe.wait_ge(ot_copied, b + 1)
                if b >= 2:
                    pe.wait_ge(proj_added, b - 1)
                for c in range(TPB):
                    last = mm(bank[b % 2][:, c * P:(c + 1) * P], OT[:, b % 2, c * P:(c + 1) * P],
                              Wout[:], start=True, stop=True)
                last.then_inc(proj_made, 1)

            pe.wait_ge(phiq_ready, NBATCH)
            numerators(0)
            numerators(1)
            for b in range(NBATCH):
                if b + 1 < NBATCH:
                    numerators(2 * b + 2)
                turn_out(b)
                if b + 1 < NBATCH:
                    numerators(2 * b + 3)
                project_out(b)

            def rows_turned(r, s, turn, first=False):
                pe.wait_ge(gathered[r], turn * 16 + 16)
                if not first:
                    pe.wait_ge(xgt_copied, s)
                tp(bank[3][:, 0:P], XG[:, r], ident).then_inc(xgt_made, 1)

            def gate_up(made, taken, n, weights, r, s, e, first=False):
                pe.wait_ge(xgt_copied, s + 1)
                if not first:
                    pe.wait_ge(taken, s)
                mm(bank[n][:], XGT[:, r], weights[:, bass.ds(e * I, I)],
                   start=True, stop=True).then_inc(made, 1)

            def hidden_turned(s, first):
                pe.wait_ge(hidden_ready, s + 1)
                if not first:
                    pe.wait_ge(ht_copied, s)
                for c in range(IC):
                    last = tp(bank[2][:, c * P:(c + 1) * P], HG[:, c * P:(c + 1) * P], ident)
                last.then_inc(ht_made, 1)

            def lower(s, e, first):
                pe.wait_ge(ht_copied, s + 1)
                if not first:
                    pe.wait_ge(y_ready, s)
                for c in range(IC):
                    last = mm(bank[4][:, 0:D], HT[:, c * P:(c + 1) * P],
                              Wd[:, bass.ds(e * I + c * D, D)], start=(c == 0), stop=(c == IC - 1))
                last.then_inc(y_made, 1)

            def experts_of(turn):
                w = pe.value_load(word[0:1, turn], min_val=0, max_val=E ** (RING + 1) - 1)
                return [pe.snap((w // E ** n) % E) for n in range(RING + 1)]

            pe.wait_ge(proj_added, NBATCH)
            pe.wait_ge(word_ready, 1)
            pe.wait_ge(gate_loaded, 16)
            pe.wait_ge(up_loaded, 16)
            pe.wait_ge(down_loaded, 16)
            rows_turned(0, 0, 0, first=True)
            rows_turned(1, 1, 0)
            ids = experts_of(slice(0, 1))
            gate_up(gate_made, silu_ready, 0, Wg, 0, 0, ids[0], first=True)
            gate_up(up_made, hidden_ready, 1, Wu, 0, 0, ids[0], first=True)

            def turn(i, first=False, last=False):
                ids = experts_of(slice(i, i + 1) if first or last else bass.ds(i, 1))
                for r in range(RING):
                    s = i * RING + r
                    ahead = (r + 1) % RING
                    more = not last or r + 1 < RING
                    if more:
                        gate_up(gate_made, silu_ready, 0, Wg, ahead, s + 1, ids[r + 1])
                    hidden_turned(s, first and r == 0)
                    if more:
                        gate_up(up_made, hidden_ready, 1, Wu, ahead, s + 1, ids[r + 1])
                    if not last or r + 2 < RING:
                        rows_turned((r + 2) % RING, s + 2, i + (r + 2) // RING)
                    lower(s, ids[r], first and r == 0)

            turn(0, first=True)
            with pe.Fori(1, NR - 1) as i:
                turn(i)
            turn(NR - 1, last=True)


def kernel(L0_attn_x, L0_attn_w_qkv, L0_attn_w_out, L0_attn_b_out, L0_ffn_router_w, L0_ffn_gate_w,
           L0_ffn_up_w, L0_ffn_down_w):
    import concourse.bacc as bacc
    from concourse.bass_utils import run_bass_kernel_spmd

    def laid(a, shape=None):
        a = np.ascontiguousarray(a)
        return a if shape is None else a.reshape(shape)

    arrays = dict(
        x=laid(L0_attn_x, (T, D)),
        wqkv=laid(np.asarray(L0_attn_w_qkv).T),
        wout=laid(np.asarray(L0_attn_w_out).T),
        bout=laid(L0_attn_b_out),
        router=laid(np.asarray(L0_ffn_router_w).T),
        gate=laid(np.asarray(L0_ffn_gate_w).transpose(2, 0, 1), (D, E * I)),
        up=laid(np.asarray(L0_ffn_up_w).transpose(2, 0, 1), (D, E * I)),
        down=laid(np.asarray(L0_ffn_down_w).reshape(E, D, IC, P).transpose(3, 0, 2, 1), (P, E * I)),
        const=constants(),
    )
    nc = bacc.Bacc("TRN2", target_bir_lowering=False, num_devices=1)
    args = [nc.dram_tensor(name, a.shape, F32, kind="ExternalInput").ap() for name, a in arrays.items()]
    out = nc.dram_tensor("out", (T, D), F32, kind="ExternalOutput").ap()
    moe_attention_block(nc, *args, out)
    r = run_bass_kernel_spmd(nc, [arrays], core_ids=[0])
    return r.results[0]["out"].reshape(NBATCH, SEQ, D)
```

```python
from contextlib import ExitStack

import numpy as np
import concourse.bass as bass
from concourse import mybir

F32 = mybir.dt.float32
F16 = mybir.dt.float16
I32 = mybir.dt.int32
U32 = mybir.dt.uint32
ALU = mybir.AluOpType
ACT = mybir.ActivationFunctionType
AX_X = mybir.AxisListType.X

P = 128
D = 128
NBATCH, SEQ = 4, 512
T = NBATCH * SEQ
NT = T // P
TPB = SEQ // P
H, HD = 16, 8
E, I = 8, 512
IC = I // P
TOP = 2
NS = (TOP * T + E * (P - 1)) // P
RING = 3
NR = NS // RING
NWORD = RING + 2
assert NR * RING == NS
NW = D + H
LN_EPS, Z_EPS = 1e-5, 1e-6
TAKEN = 1e30
NO_ROW = 2 * TOP * T

_SIZES = dict(ident=P, upper=P, ones=P, prefix=P, total=E, rev=E, tiles=NS, lanes=P, steps=NT,
              below=E * E, code=TOP * NT, heads=D, headsel=H)
COL, _at = {}, 0
for _name, _n in _SIZES.items():
    COL[_name] = (_at, _at + _n)
    _at += _n
NCONST = _at
WARM = 4


def constants():
    c = np.zeros((P, NCONST), np.float32)
    p = np.arange(P)

    def put(name, value):
        c[:, COL[name][0]:COL[name][1]] = value

    put("ident", np.eye(P))
    put("upper", p[:, None] < p[None, :])
    put("ones", 1.0)
    tile, expert = p // E, p % E
    put("prefix", (expert[:, None] == expert) & (tile[:, None] < tile))
    put("total", expert[:, None] == np.arange(E))
    put("rev", E - np.arange(E))
    put("tiles", np.arange(NS))
    put("lanes", p)
    put("steps", P * np.arange(NT))
    put("below", (np.arange(E)[None, :] < np.arange(E)[:, None]).reshape(-1))
    token = P * np.arange(NT)[None, :] + p[:, None] + 1
    put("code", np.concatenate([-token, token], 1))
    put("heads", (p[:, None] // HD) == (p[None, :] // HD))
    put("headsel", (p[:, None] // HD) == np.arange(H))
    return c


def moe_attention_block(nc, x, wqkv, wout, bout, router, gate, up, down, const, out):
    with ExitStack() as ctx:
        def sb(name, shape, dt=F32):
            return ctx.enter_context(nc.sbuf_tensor(name, shape, dt))

        def sem(name):
            return ctx.enter_context(nc.semaphore(name))

        bank = [ctx.enter_context(nc.psum_tensor(f"bank{n}", [P, 512], F32)) for n in range(8)]
        xn_rows = nc.dram_tensor("xn_rows", (T, D), F32, kind="Internal").ap()
        expert_rows = nc.dram_tensor("expert_rows", (TOP * T, D), F32, kind="Internal").ap()

        X = sb("X", [P, NT, D])
        XN = sb("XN", [P, NT, D])
        XNT = sb("XNT", [P, T])
        Wqkv = sb("Wqkv", [P, 3 * D])
        Wout = sb("Wout", [P, D])
        Bout = sb("Bout", [P, D])
        Wr = sb("Wr", [P, E])
        Wg = sb("Wg", [P, E * I])
        Wu = sb("Wu", [P, E * I])
        Wd = sb("Wd", [P, E * I])
        K = sb("K", [P, NCONST])
        stats = sb("stats", [P, NT, 6])
        mv = sb("mv", [P, NT, 2])
        var = sb("var", [P, NT])
        std = sb("std", [P, NT])
        rstd = sb("rstd", [P, NT])
        newt = sb("newt", [P, NT])
        rs = sb("rs", [P, NT])
        ek = sb("ek", [P, 2, SEQ])
        rk = sb("rk", [P, 2, SEQ])
        eq = sb("eq", [P, 2, SEQ])
        rq = sb("rq", [P, 2, SEQ])
        PK = sb("PK", [P, NBATCH, SEQ])
        PQ = sb("PQ", [P, NBATCH, SEQ])
        V1 = sb("V1", [P, NT, D + 1])
        KVR = sb("KVR", [P, NBATCH, NW])
        den = sb("den", [P, 2, H])
        z = sb("z", [P, 2, H])
        O = sb("O", [P, NT, D])
        OT = sb("OT", [P, 2, SEQ])
        XB = sb("XB", [P, NT, D])
        top = sb("top", [P, TOP, NT])
        L2 = sb("L2", [P, NT, E])
        Ls = sb("Ls", [P, NT, E])
        Ex = sb("Ex", [P, NT, E])
        ssum = sb("ssum", [P, NT])
        rsum = sb("rsum", [P, NT])
        Pr = sb("Pr", [P, NT, E])
        cand = sb("cand", [P, NT, E])
        mark = sb("mark", [P, NT])
        OH = sb("OH", [P, TOP, NT, E])
        M16 = sb("M16", [P, NT * E], F16)
        psum2 = sb("psum2", [P, NT])
        WT = sb("WT", [P, TOP, NT, E])
        WTs = sb("WTs", [P, NT, E])
        upper16 = sb("upper16", [P, P], F16)
        ones16 = sb("ones16", [P, P], F16)
        prefix16 = sb("prefix16", [P, P], F16)
        total16 = sb("total16", [P, E], F16)
        tot16 = sb("tot16", [P, P], F16)
        cnt = sb("cnt", [P, E])
        gt = sb("gt", [P, E, NT])
        ntile = sb("ntile", [P, E])
        basep = sb("basep", [P, E, E])
        base = sb("base", [P, E])
        slot = sb("slot", [P, NT, E])
        pos = sb("pos", [P, TOP, NT])
        posi = sb("posi", [P, TOP * NT], I32)
        hilo = sb("hilo", [P, 2, TOP * NT], I32)
        hilo16 = sb("hilo16", [P, 2, TOP * NT], F16)
        tiles16 = sb("tiles16", [P, NS, TOP * NT], F16)
        lanes16 = sb("lanes16", [P, P, TOP * NT], F16)
        code16 = sb("code16", [P, TOP * NT], F16)
        OHcode = sb("OHcode", [P, NS, TOP * NT], F16)
        OHlo = sb("OHlo", [P, P, TOP * NT], F16)
        code = sb("code_of_slot", [P, NS])
        row1 = sb("row1", [P, NS])
        second = sb("second", [P, NS])
        pad = sb("pad", [P, NS])
        IDX = sb("IDX", [P, NS, 2], U32)
        ge = sb("ge", [P, NS, E])
        eid = sb("eid", [P, NS + 2])
        words = sb("words", [P, NR])
        word = sb("word", [P, NR], I32)
        sumw = sb("sumw", [P, E])
        meanw = sb("meanw", [P, E])
        scale = sb("scale", [P, NS])
        gidx = sb("gidx", [P, RING, 1], U32)
        sidx = sb("sidx", [P, RING, 1], U32)
        XG = sb("XG", [P, RING, D])
        XGT = sb("XGT", [P, RING, P])
        SG = sb("SG", [P, I])
        HG = sb("HG", [P, I])
        HT = sb("HT", [P, I])
        Y = sb("Y", [P, RING, D])
        Y01 = sb("Y01", [P, TOP, NT, D])

        def k_(name, n=None):
            a, b = COL[name]
            return K[:, a:b]

        def over_tiles(ap, n=NT):
            return ap.unsqueeze(1).to_broadcast([P, n, E])

        def over_experts(ap, n=NT):
            return ap.unsqueeze(2).to_broadcast([P, n, E])

        x_loaded = [sem(f"x_loaded{q}") for q in range(NBATCH)]
        const_loaded = sem("const_loaded")
        attn_weights_loaded = sem("attn_weights_loaded")
        gate_loaded = sem("gate_loaded")
        up_loaded = sem("up_loaded")
        down_loaded = sem("down_loaded")
        dve_step = sem("dve_step")
        var_ready = sem("var_ready")
        std_ready = sem("std_ready")
        xn_ready = sem("xn_ready")
        xn_stored = sem("xn_stored")
        xt_made = sem("xt_made")
        xt_copied = sem("xt_copied")
        consts16 = sem("consts16")
        logits_made = sem("logits_made")
        shifted = sem("shifted")
        exp_ready = sem("exp_ready")
        chosen = sem("chosen")
        tot_made = sem("tot_made")
        tot_copied = sem("tot_copied")
        rank_made = sem("rank_made")
        weights_ready = sem("weights_ready")
        sumw_made = sem("sumw_made")
        tables_ready = sem("tables_ready")
        onehot_ready = sem("onehot_ready")
        code_made = sem("code_made")
        index_ready = sem("index_ready")
        word_ready = sem("word_ready")
        mean_step = sem("mean_step")
        den_ready = sem("den_ready")
        k_made = sem("k_made")
        v_made = sem("v_made")
        q_made = sem("q_made")
        k_taken = sem("k_taken")
        negative = sem("negative")
        k_terms = sem("k_terms")
        q_terms = sem("q_terms")
        v_taken = sem("v_taken")
        q_taken = sem("q_taken")
        phik_ready = sem("phik_ready")
        phiq_ready = sem("phiq_ready")
        v_ones = sem("v_ones")
        kv_made = sem("kv_made")
        kv_ready = sem("kv_ready")
        num_made = sem("num_made")
        o_ready = sem("o_ready")
        ot_made = sem("ot_made")
        ot_copied = sem("ot_copied")
        proj_made = sem("proj_made")
        proj_added = sem("proj_added")
        xb_ready = sem("xb_ready")
        gathered = [sem(f"gathered{r}") for r in range(RING)]
        scattered = [sem(f"scattered{r}") for r in range(RING)]
        indices_copied = sem("indices_copied")
        xgt_made = sem("xgt_made")
        xgt_copied = sem("xgt_copied")
        gate_made = sem("gate_made")
        up_made = sem("up_made")
        silu_ready = sem("silu_ready")
        hidden_ready = sem("hidden_ready")
        ht_made = sem("ht_made")
        ht_copied = sem("ht_copied")
        y_made = sem("y_made")
        y_ready = sem("y_ready")
        first_loaded = [sem(f"first_loaded{q}") for q in range(NBATCH)]
        second_loaded = [sem(f"second_loaded{q}") for q in range(NBATCH)]
        final_step = sem("final_step")
        final_ready = sem("final_ready")
        out_stored = sem("out_stored")

        x_d = x.rearrange("(q c p) d -> q p c d", p=P, c=TPB)
        xn_d = xn_rows.rearrange("(q c p) d -> q p c d", p=P, c=TPB)
        er_d = expert_rows.rearrange("(k q c p) d -> k q p c d", k=TOP, p=P, c=TPB)
        out_d = out.rearrange("(q c p) d -> q p c d", p=P, c=TPB)

        def quarter(buf, q):
            return buf[:, q * TPB:(q + 1) * TPB, :]

        block = ctx.enter_context(nc.Block())

        @block.sync
        def _(sp):
            for q in range(0, NBATCH, 2):
                sp.dma_start(quarter(X, q), x_d[q]).then_inc(x_loaded[q], 16)
            sp.dma_start(Wr[:], router).then_inc(attn_weights_loaded, 16)
            sp.dma_start(Wqkv[:], wqkv).then_inc(attn_weights_loaded, 16)
            sp.dma_start(Wout[:], wout).then_inc(attn_weights_loaded, 16)
            sp.dma_start(Bout[:], bout.partition_broadcast(P)).then_inc(attn_weights_loaded, 16)
            sp.dma_start(Wg[:], gate).then_inc(gate_loaded, 16)
            sp.dma_start(Wu[:], up).then_inc(up_loaded, 16)
            sp.dma_start(Wd[:], down).then_inc(down_loaded, 16)
            for r in range(RING):
                sp.wait_ge(scattered[r], 16 * NR)
            for q in range(NBATCH):
                sp.dma_start(quarter(Y01[:, 0], q), er_d[0, q]).then_inc(first_loaded[q], 16)
            for q in range(NBATCH):
                sp.wait_ge(final_ready, q + 1)
                sp.dma_start(out_d[q], quarter(X, q)).then_inc(out_stored, 16)
            sp.wait_ge(out_stored, 16 * NBATCH)

        @block.scalar
        def _(act):
            for q in range(1, NBATCH, 2):
                act.dma_start(quarter(X, q), x_d[q]).then_inc(x_loaded[q], 16)
            act.dma_start(K[:], const).then_inc(const_loaded, 16)
            act.wait_ge(var_ready, 1)
            nc.scalar.activation(std[:], var[:], ACT.Sqrt).then_inc(std_ready, 1)
            for q in range(NBATCH):
                act.wait_ge(xt_made, q + 1)
                nc.scalar.copy(XNT[:, q * SEQ:(q + 1) * SEQ], bank[q % 2][:]).then_inc(xt_copied, 1)
                act.wait_ge(xn_ready, (q + 1) * TPB)
                act.dma_start(xn_d[q], quarter(XN, q)).then_inc(xn_stored, 16)
            act.wait_ge(shifted, 1)
            nc.scalar.activation(Ex[:], Ls[:], ACT.Exp).then_inc(exp_ready, 1)
            taken = [0]

            def phi_terms(source, ez, rz, done, done_value, b):
                if b >= 2:
                    act.wait_ge(done_value, b - 1)
                nc.scalar.activation(ez[:, b % 2], source, ACT.Relu, scale=-1.0).then_inc(negative, 1)
                taken[0] += 1
                nc.scalar.activation(rz[:, b % 2], source, ACT.Relu).then_inc(done[0], 1)
                act.wait_ge(negative, taken[0])
                nc.scalar.activation(ez[:, b % 2], ez[:, b % 2], ACT.Exp, scale=-1.0).then_inc(done[1], 1)

            for b in range(NBATCH):
                act.wait_ge(k_made, b + 1)
                phi_terms(bank[0][:], ek, rk, (k_taken, k_terms), phik_ready, b)
                act.wait_ge(v_made, b + 1)
                nc.scalar.copy(V1[:, b * TPB:(b + 1) * TPB, 0:D],
                               bank[1][:].rearrange("p (c d) -> p c d", d=D)).then_inc(v_taken, 1)
                act.wait_ge(q_made, b + 1)
                phi_terms(bank[2][:], eq, rq, (q_taken, q_terms), phiq_ready, b)
            nc.scalar.preload_act_table(ACT.Silu)
            for b in range(NBATCH):
                act.wait_ge(ot_made, b + 1)
                if b >= 2:
                    act.wait_ge(proj_made, b - 1)
                nc.scalar.copy(OT[:, b % 2], bank[2][:]).then_inc(ot_copied, 1)

            def activate(s, first=False):
                act.wait_ge(gate_made, s + 1)
                if not first:
                    act.wait_ge(hidden_ready, s)
                nc.scalar.activation(SG[:], bank[0][:], ACT.Silu).then_inc(silu_ready, 1)
                act.wait_ge(ht_made, s + 1)
                if not first:
                    act.wait_ge(y_made, s)
                nc.scalar.copy(HT[:], bank[2][:]).then_inc(ht_copied, 1)

            activate(0, first=True)
            with act.Fori(1, NS) as s:
                activate(s)

            for q in range(NBATCH):
                if q == 0:
                    for r in range(RING):
                        act.wait_ge(scattered[r], 16 * NR)
                act.dma_start(quarter(Y01[:, 1], q), er_d[1, q]).then_inc(second_loaded[q], 16)

        @block.gpsimd
        def _(pool):
            nc.gpsimd.memset(V1[:, :, D:D + 1], 1.0).then_inc(v_ones, 1)
            pool.wait_ge(const_loaded, 16)
            nc.gpsimd.tensor_copy(upper16[:], k_("upper"))
            nc.gpsimd.tensor_copy(ones16[:], k_("ones"))
            nc.gpsimd.tensor_copy(prefix16[:], k_("prefix"))
            nc.gpsimd.tensor_copy(total16[:], k_("total")).then_inc(consts16, 1)
            pool.wait_ge(consts16, 1)
            for q in range(NBATCH):
                pool.wait_ge(x_loaded[q], 16)
            pool.wait_ge(attn_weights_loaded, 64)
            nc.gpsimd.tensor_tensor(XB[:], X[:], Bout[:].unsqueeze(1).to_broadcast([P, NT, D]),
                                    ALU.add).then_inc(xb_ready, 1)

            def phi(b):
                for terms, ez, rz, to, done in ((k_terms, ek, rk, PK, phik_ready),
                                                (q_terms, eq, rq, PQ, phiq_ready)):
                    pool.wait_ge(terms, b + 1)
                    nc.gpsimd.tensor_tensor(to[:, b], ez[:, b % 2], rz[:, b % 2], ALU.add).then_inc(done, 1)

            for b in range(NBATCH):
                phi(b)

            pool.wait_ge(index_ready, 1)
            pool.wait_ge(xn_stored, 16 * NBATCH)

            def gather(r, tile):
                nc.gpsimd.tensor_copy(gidx[:, r], IDX[:, tile, 0:1]).then_inc(indices_copied, 1)
                pool.wait_ge(indices_copied, 1)
                nc.gpsimd.indirect_dma_start(
                    XG[:, r], None, xn_rows, bass.IndirectOffsetOnAxis(gidx[:, r], 0)).then_inc(gathered[r], 16)
                pool.sem_clear(indices_copied)

            def scatter(r, tile):
                nc.gpsimd.tensor_copy(sidx[:, r], IDX[:, tile, 1:2]).then_inc(indices_copied, 1)
                pool.wait_ge(indices_copied, 1)
                nc.gpsimd.indirect_dma_start(
                    expert_rows, bass.IndirectOffsetOnAxis(sidx[:, r], 0), Y[:, r], None,
                    bounds_check=TOP * T - 1, oob_is_err=False).then_inc(scattered[r], 16)
                pool.sem_clear(indices_copied)

            for r in range(RING):
                gather(r, slice(r, r + 1))
            with pool.Fori(0, NR - 1) as i:
                for r in range(RING):
                    s = i * RING + r
                    pool.wait_ge(xgt_made, s + 1)
                    gather(r, bass.ds(s + RING, 1))
                    pool.wait_ge(y_ready, s + 1)
                    scatter(r, bass.ds(s, 1))
            for r in range(RING):
                s = NS - RING + r
                pool.wait_ge(y_ready, s + 1)
                scatter(r, slice(s, s + 1))
            for r in range(RING):
                pool.wait_ge(scattered[r], 16 * NR)

        @block.vector
        def _(dve):
            steps = [0]

            def step(ins):
                steps[0] += 1
                ins.then_inc(dve_step, 1)
                dve.wait_ge(dve_step, steps[0])

            v = nc.vector
            for q in range(NBATCH):
                dve.wait_ge(x_loaded[q], 16)
                for t in range(q * TPB, (q + 1) * TPB):
                    last = v.bn_stats(stats[:, t], X[:, t])
            step(last)
            for t in range(NT):
                last = v.bn_aggr(mv[:, t], stats[:, t])
            step(last)
            v.tensor_scalar(var[:], mv[:, :, 1], LN_EPS, None, ALU.add).then_inc(var_ready, 1)
            dve.wait_ge(std_ready, 1)
            step(v.reciprocal(rstd[:], std[:]))
            step(v.tensor_tensor(newt[:], rstd[:], rstd[:], ALU.mult))
            step(v.tensor_tensor(newt[:], newt[:], var[:], ALU.mult))
            step(v.tensor_scalar(newt[:], newt[:], -0.5, 1.5, ALU.mult, ALU.add))
            step(v.tensor_tensor(rs[:], rstd[:], newt[:], ALU.mult))
            for t in range(NT):
                v.tensor_scalar(XN[:, t], X[:, t], mv[:, t, 0:1], rs[:, t:t + 1],
                                ALU.subtract, ALU.mult).then_inc(xn_ready, 1)

            dve.wait_ge(const_loaded, 16)
            v.tensor_copy(tiles16[:], k_("tiles").unsqueeze(2).to_broadcast([P, NS, TOP * NT]))
            v.tensor_copy(code16[:], k_("code"))
            v.tensor_copy(lanes16[:], k_("lanes").unsqueeze(2).to_broadcast(
                [P, P, TOP * NT])).then_inc(tables_ready, 1)

            dve.wait_ge(logits_made, NBATCH)
            L = bank[3][:, 0:NT * E].rearrange("p (t e) -> p t e", e=E)
            step(v.tensor_reduce(top[:, 0], L, AX_X, ALU.max))

            def choose(k, logits):
                step(v.tensor_tensor(cand[:], logits, over_experts(top[:, k]), ALU.is_ge))
                step(v.tensor_tensor(cand[:], cand[:], over_tiles(k_("rev")), ALU.mult))
                step(v.tensor_reduce(mark[:], cand[:], AX_X, ALU.max))
                step(v.tensor_tensor(OH[:, k], over_tiles(k_("rev")), over_experts(mark[:]), ALU.is_equal))

            choose(0, L)
            step(v.scalar_tensor_tensor(L2[:], OH[:, 0], -TAKEN, L, ALU.mult, ALU.add))
            step(v.tensor_reduce(top[:, 1], L2[:], AX_X, ALU.max))
            choose(1, L2[:])
            v.tensor_tensor(M16[:].rearrange("p (t e) -> p t e", e=E), OH[:, 0], OH[:, 1],
                            ALU.add).then_inc(chosen, 1)

            v.tensor_tensor(Ls[:], L, over_experts(top[:, 0]), ALU.subtract).then_inc(shifted, 1)
            dve.wait_ge(tot_made, 1)
            v.tensor_copy(tot16[:], bank[7][:, 256:384]).then_inc(tot_copied, 1)
            dve.wait_ge(exp_ready, 1)
            step(v.tensor_reduce(ssum[:], Ex[:], AX_X, ALU.add))
            step(v.reciprocal(rsum[:], ssum[:]))
            step(v.tensor_tensor(Pr[:], Ex[:], over_experts(rsum[:]), ALU.mult))
            step(v.tensor_tensor(WT[:], OH[:], Pr[:].unsqueeze(1).to_broadcast([P, TOP, NT, E]), ALU.mult))
            step(v.tensor_tensor(WTs[:], WT[:, 0], WT[:, 1], ALU.add))
            step(v.tensor_reduce(psum2[:], WTs[:], AX_X, ALU.add))
            step(v.reciprocal(psum2[:], psum2[:]))
            v.tensor_tensor(WTs[:], WTs[:], over_experts(psum2[:]), ALU.mult).then_inc(weights_ready, 1)

            dve.wait_ge(rank_made, 1)
            v.tensor_copy(cnt[:], bank[4][:, P:P + E])
            step(v.tensor_tensor(gt[:], bank[4][:, P:P + E].unsqueeze(2).to_broadcast([P, E, NT]),
                                 k_("steps").unsqueeze(1).to_broadcast([P, E, NT]), ALU.is_gt))
            step(v.tensor_reduce(ntile[:], gt[:], AX_X, ALU.add))
            step(v.tensor_tensor(basep[:], ntile[:].unsqueeze(1).to_broadcast([P, E, E]),
                                 k_("below").rearrange("p (a b) -> p a b", b=E), ALU.mult))
            step(v.tensor_reduce(base[:], basep[:], AX_X, ALU.add))
            step(v.scalar_tensor_tensor(slot[:], over_tiles(base[:]), float(P),
                                        bank[4][:, 0:P].rearrange("p (t e) -> p t e", e=E),
                                        ALU.mult, ALU.add))
            step(v.tensor_tensor(WT[:], OH[:], slot[:].unsqueeze(1).to_broadcast([P, TOP, NT, E]), ALU.mult))
            step(v.tensor_reduce(pos[:], WT[:], AX_X, ALU.add))
            step(v.tensor_copy(posi[:], pos[:].rearrange("p k t -> p (k t)")))
            v.tensor_scalar(hilo[:, 0], posi[:], 7, None, ALU.arith_shift_right)
            step(v.tensor_scalar(hilo[:, 1], posi[:], P - 1, None, ALU.bitwise_and))
            step(v.tensor_copy(hilo16[:], hilo[:]))
            dve.wait_ge(tables_ready, 1)
            step(v.tensor_tensor(OHcode[:], tiles16[:], hilo16[:, 0:1].to_broadcast([P, NS, TOP * NT]),
                                 ALU.is_equal))
            v.tensor_tensor(OHcode[:], OHcode[:], code16[:].unsqueeze(1).to_broadcast([P, NS, TOP * NT]),
                            ALU.mult)
            v.tensor_tensor(OHlo[:], lanes16[:], hilo16[:, 1:2].to_broadcast([P, P, TOP * NT]),
                            ALU.is_equal).then_inc(onehot_ready, 1)

            dve.wait_ge(code_made, 1)
            step(v.tensor_copy(code[:], bank[3][:, P:P + NS]))
            step(v.scalar_tensor_tensor(row1[:], code[:], -1.0, code[:], ALU.mult, ALU.max))
            v.tensor_scalar(IDX[:, :, 0], row1[:], -1.0, 0.0, ALU.add, ALU.max)
            v.tensor_scalar(second[:], code[:], 0.0, float(T), ALU.is_gt, ALU.mult)
            step(v.tensor_scalar(pad[:], code[:], 0.0, float(NO_ROW), ALU.is_equal, ALU.mult))
            step(v.scalar_tensor_tensor(row1[:], row1[:], -1.0, second[:], ALU.add, ALU.add))
            v.tensor_tensor(IDX[:, :, 1], row1[:], pad[:], ALU.add).then_inc(index_ready, 1)

            step(v.tensor_tensor(ge[:], k_("tiles").unsqueeze(2).to_broadcast([P, NS, E]),
                                 over_tiles(base[:], NS), ALU.is_ge))
            step(v.memset(eid[:], 0.0))
            step(v.tensor_reduce(eid[:, 1:NS + 1], ge[:], AX_X, ALU.add))
            step(v.tensor_scalar(eid[:, 1:NS + 1], eid[:, 1:NS + 1], -1.0, None, ALU.add))

            def nth(m):
                return eid[:, m:m + (NR - 1) * RING + 1:RING]

            step(v.tensor_copy(words[:], nth(NWORD - 1)))
            for m in range(NWORD - 2, -1, -1):
                step(v.scalar_tensor_tensor(words[:], words[:], float(E), nth(m), ALU.mult, ALU.add))
            v.tensor_copy(word[:], words[:]).then_inc(word_ready, 1)

            def mean_weight(j):
                if j == 0:
                    dve.wait_ge(sumw_made, 1)
                    v.tensor_reduce(sumw[:], bank[7][:, 0:NT * E].rearrange("p (t e) -> p e t", e=E),
                                    AX_X, ALU.add).then_inc(mean_step, 1)
                    return
                dve.wait_ge(mean_step, j)
                if j == 1:
                    ins = v.tensor_scalar(cnt[:], cnt[:], 1.0, None, ALU.max)
                elif j == 2:
                    ins = v.reciprocal(cnt[:], cnt[:])
                elif j == 3:
                    ins = v.tensor_tensor(meanw[:], sumw[:], cnt[:], ALU.mult)
                elif j == 4:
                    ins = v.tensor_scalar(eid[:, 1:NS + 1], eid[:, 1:NS + 1], -1.0, float(E), ALU.mult, ALU.add)
                elif j == 5:
                    ins = v.tensor_tensor(ge[:], over_tiles(k_("rev"), NS), over_experts(eid[:, 1:NS + 1], NS),
                                          ALU.is_equal)
                elif j == 6:
                    ins = v.tensor_tensor(ge[:], ge[:], over_tiles(meanw[:], NS), ALU.mult)
                else:
                    ins = v.tensor_reduce(scale[:], ge[:], AX_X, ALU.add)
                ins.then_inc(mean_step, 1)

            mean_weight(0)
            for b in range(NBATCH):
                dve.wait_ge(kv_made, NBATCH)
                kv = bank[5][:, b * (D + 1):(b + 1) * (D + 1)] if b < 3 else bank[6][:, 0:D + 1]
                v.tensor_tensor(KVR[:, b, 0:D], kv[:, 0:D], k_("heads"), ALU.mult)
                v.tensor_tensor(KVR[:, b, D:NW], kv[:, D:D + 1].to_broadcast([P, H]), k_("headsel"),
                                ALU.mult).then_inc(kv_ready, 1)
            def add_projection(b):
                if b == 0:
                    dve.wait_ge(xb_ready, 1)
                dve.wait_ge(proj_made, b + 1)
                v.tensor_tensor(quarter(X, b), quarter(XB, b),
                                bank[b % 2][:].rearrange("p (c d) -> p c d", d=D),
                                ALU.add).then_inc(proj_added, 1)

            for j in range(NT // 2):
                dve.wait_ge(num_made, j + 1)
                nd = bank[6 + j % 2][:, 0:2 * NW].rearrange("p (c n) -> p c n", n=NW)
                v.tensor_scalar(den[:], nd[:, :, D:NW], Z_EPS, None, ALU.add).then_inc(den_ready, 1)
                if j:
                    mean_weight(j)
                dve.wait_ge(den_ready, j + 1)
                step(v.reciprocal(z[:], den[:]))
                v.tensor_tensor(O[:, 2 * j:2 * j + 2].rearrange("p c (h d) -> p c h d", d=HD),
                                nd[:, :, 0:D].rearrange("p c (h d) -> p c h d", d=HD),
                                z[:].unsqueeze(3).to_broadcast([P, 2, H, HD]),
                                ALU.mult).then_inc(o_ready, 1)
                if j % 2 == 1 and j >= 3:
                    add_projection(j // 2 - 1)
            add_projection(NBATCH - 1)

            def rows_copied(n, s):
                dve.wait_ge(xgt_made, s + 1)
                v.tensor_copy(XGT[:, n], bank[3][:, 0:P]).then_inc(xgt_copied, 1)

            def hidden(s, first=False):
                dve.wait_ge(silu_ready, s + 1)
                dve.wait_ge(up_made, s + 1)
                if not first:
                    dve.wait_ge(ht_made, s)
                v.tensor_tensor(HG[:], SG[:], bank[1][:], ALU.mult).then_inc(hidden_ready, 1)

            def result(r, s, turn, tile):
                dve.wait_ge(y_made, s + 1)
                if turn is not None:
                    dve.wait_ge(scattered[r], turn * 16)
                v.tensor_scalar(Y[:, r], bank[4][:, 0:D], scale[:, tile], None,
                                ALU.mult).then_inc(y_ready, 1)

            def turn(i, first=False, last=False):
                for r in range(RING):
                    s = i * RING + r
                    if not last or r + 2 < RING:
                        rows_copied((r + 2) % RING, s + 2)
                    if not last or r + 1 < RING:
                        hidden(s + 1)
                    result(r, s, None if first else i,
                           slice(s, s + 1) if first or last else bass.ds(s, 1))

            rows_copied(0, 0)
            rows_copied(1, 1)
            dve.wait_ge(mean_step, NT // 2)
            hidden(0, first=True)
            turn(0, first=True)
            with dve.Fori(1, NR - 1) as i:
                turn(i)
            turn(NR - 1, last=True)

            for q in range(NBATCH):
                dve.wait_ge(first_loaded[q], 16)
                v.tensor_tensor(quarter(X, q), quarter(X, q), quarter(Y01[:, 0], q),
                                ALU.add).then_inc(final_step, 1)
                dve.wait_ge(final_step, q + 1)
                dve.wait_ge(second_loaded[q], 16)
                v.tensor_tensor(quarter(X, q), quarter(X, q), quarter(Y01[:, 1], q),
                                ALU.add).then_inc(final_ready, 1)

        @block.tensor
        def _(pe):
            mm, tp = nc.tensor.matmul, nc.tensor.transpose
            ident = k_("ident")
            pe.wait_ge(const_loaded, 16)
            for _ in range(WARM):
                mm(bank[7][:], ident, K[:, 0:512], start=True, stop=True)

            def turn_in(q):
                if q >= 2:
                    pe.wait_ge(xt_copied, q - 1)
                for c in range(TPB):
                    t = q * TPB + c
                    pe.wait_ge(xn_ready, t + 1)
                    last = tp(bank[q % 2][:, c * P:(c + 1) * P], XN[:, t], ident)
                last.then_inc(xt_made, 1)

            def logits(q):
                pe.wait_ge(attn_weights_loaded, 64)
                pe.wait_ge(xt_copied, q + 1)
                for t in range(q * TPB, (q + 1) * TPB):
                    last = mm(bank[3][:, t * E:(t + 1) * E], XNT[:, t * P:(t + 1) * P], Wr[:],
                              start=True, stop=True)
                last.then_inc(logits_made, 1)

            turn_in(0)
            for q in range(1, NBATCH):
                turn_in(q)
                logits(q - 1)
            logits(NBATCH - 1)

            def kv_sum(b):
                pe.wait_ge(phik_ready, b + 1)
                pe.wait_ge(v_taken, b + 1)
                o = bank[5][:, b * (D + 1):(b + 1) * (D + 1)] if b < 3 else bank[6][:, 0:D + 1]
                for c in range(TPB):
                    last = mm(o, PK[:, b, c * P:(c + 1) * P], V1[:, b * TPB + c],
                              start=(c == 0), stop=(c == TPB - 1))
                last.then_inc(kv_made, 1)

            def project_in(b):
                for n, taken, made in ((1, k_taken, k_made), (2, v_taken, v_made)):
                    if b:
                        pe.wait_ge(taken, b)
                    for c in range(TPB):
                        t = b * TPB + c
                        last = mm(bank[n - 1][:, c * P:(c + 1) * P], XNT[:, t * P:(t + 1) * P],
                                  Wqkv[:, n * D:(n + 1) * D], start=True, stop=True)
                    last.then_inc(made, 1)
                if b:
                    pe.wait_ge(q_taken, b)
                mm(bank[2][:], Wqkv[:, 0:D], XNT[:, b * SEQ:(b + 1) * SEQ],
                   start=True, stop=True).then_inc(q_made, 1)

            project_in(0)
            pe.wait_ge(chosen, 1)
            pe.wait_ge(consts16, 1)
            mm(bank[7][:, 256:384], M16[:], ones16[:], start=True, stop=True).then_inc(tot_made, 1)
            mm(bank[4][:, 0:P], upper16[:], M16[:], start=True, stop=False)
            pe.wait_ge(tot_copied, 1)
            mm(bank[4][:, 0:P], tot16[:], prefix16[:], start=False, stop=True)
            mm(bank[4][:, P:P + E], tot16[:], total16[:], start=True, stop=True).then_inc(rank_made, 1)
            project_in(1)
            kv_sum(0)
            project_in(2)
            pe.wait_ge(weights_ready, 1)
            mm(bank[7][:, 0:NT * E], k_("ones"), WTs[:].rearrange("p t e -> p (t e)"),
               start=True, stop=True).then_inc(sumw_made, 1)
            kv_sum(1)
            pe.wait_ge(onehot_ready, 1)
            for c in range(TOP * NT):
                last = mm(bank[3][:, P:P + NS], OHlo[:, :, c], OHcode[:, :, c],
                          start=(c == 0), stop=(c == TOP * NT - 1))
            last.then_inc(code_made, 1)
            project_in(3)
            kv_sum(2)
            kv_sum(3)

            def numerators(j):
                if j == 0:
                    pe.wait_ge(kv_ready, NBATCH)
                if j >= 2:
                    pe.wait_ge(o_ready, j - 1)
                for c in range(2):
                    t = 2 * j + c
                    b = t // TPB
                    last = mm(bank[6 + j % 2][:, c * NW:(c + 1) * NW],
                              PQ[:, b, (t % TPB) * P:(t % TPB + 1) * P], KVR[:, b],
                              start=True, stop=True)
                last.then_inc(num_made, 1)

            def turn_out(b):
                pe.wait_ge(o_ready, 2 * b + 2)
                if b:
                    pe.wait_ge(ot_copied, b)
                for c in range(TPB):
                    last = tp(bank[2][:, c * P:(c + 1) * P], O[:, b * TPB + c], ident)
                last.then_inc(ot_made, 1)

            def project_out(b):
                pe.wait_ge(ot_copied, b + 1)
                if b >= 2:
                    pe.wait_ge(proj_added, b - 1)
                for c in range(TPB):
                    last = mm(bank[b % 2][:, c * P:(c + 1) * P], OT[:, b % 2, c * P:(c + 1) * P],
                              Wout[:], start=True, stop=True)
                last.then_inc(proj_made, 1)

            pe.wait_ge(phiq_ready, NBATCH)
            numerators(0)
            numerators(1)
            for b in range(NBATCH):
                if b + 1 < NBATCH:
                    numerators(2 * b + 2)
                turn_out(b)
                if b + 1 < NBATCH:
                    numerators(2 * b + 3)
                project_out(b)

            def rows_turned(r, s, turn, first=False):
                pe.wait_ge(gathered[r], turn * 16 + 16)
                if not first:
                    pe.wait_ge(xgt_copied, s)
                tp(bank[3][:, 0:P], XG[:, r], ident).then_inc(xgt_made, 1)

            def gate_up(made, taken, n, weights, r, s, e, first=False):
                pe.wait_ge(xgt_copied, s + 1)
                if not first:
                    pe.wait_ge(taken, s)
                mm(bank[n][:], XGT[:, r], weights[:, bass.ds(e * I, I)],
                   start=True, stop=True).then_inc(made, 1)

            def hidden_turned(s, first):
                pe.wait_ge(hidden_ready, s + 1)
                if not first:
                    pe.wait_ge(ht_copied, s)
                for c in range(IC):
                    last = tp(bank[2][:, c * P:(c + 1) * P], HG[:, c * P:(c + 1) * P], ident)
                last.then_inc(ht_made, 1)

            def lower(s, e, first=False):
                pe.wait_ge(ht_copied, s + 1)
                if not first:
                    pe.wait_ge(y_ready, s)
                for c in range(IC):
                    last = mm(bank[4][:, 0:D], HT[:, c * P:(c + 1) * P],
                              Wd[:, bass.ds(e * I + c * D, D)], start=(c == 0), stop=(c == IC - 1))
                last.then_inc(y_made, 1)

            def experts_of(n):
                w = pe.value_load(word[0:1, n], min_val=0, max_val=E ** NWORD - 1)
                return [(w // E ** m) % E for m in range(NWORD)]

            pe.wait_ge(proj_added, NBATCH)
            pe.wait_ge(word_ready, 1)
            pe.wait_ge(gate_loaded, 16)
            pe.wait_ge(up_loaded, 16)
            pe.wait_ge(down_loaded, 16)
            rows_turned(0, 0, 0, first=True)
            rows_turned(1, 1, 0)

            def turn(i, first=False, last=False):
                ids = experts_of(slice(i, i + 1) if first or last else bass.ds(i, 1))
                if first:
                    gate_up(gate_made, silu_ready, 0, Wg, 0, 0, ids[1], first=True)
                    gate_up(up_made, hidden_ready, 1, Wu, 0, 0, ids[1], first=True)
                else:
                    rows_turned(1, i * RING + 1, i)
                    lower(i * RING - 1, ids[0])
                for r in range(RING):
                    s = i * RING + r
                    ahead = (r + 1) % RING
                    more = not last or r + 1 < RING
                    if more:
                        gate_up(gate_made, silu_ready, 0, Wg, ahead, s + 1, ids[r + 2])
                    hidden_turned(s, first and r == 0)
                    if more:
                        gate_up(up_made, hidden_ready, 1, Wu, ahead, s + 1, ids[r + 2])
                    if r + 1 < RING and (not last or r + 2 < RING):
                        rows_turned((r + 2) % RING, s + 2, i + (r + 2) // RING)
                    if last or r + 1 < RING:
                        lower(s, ids[r + 1], first and r == 0)

            turn(0, first=True)
            with pe.Fori(1, NR - 1) as i:
                turn(i)
            turn(NR - 1, last=True)


def kernel(L0_attn_x, L0_attn_w_qkv, L0_attn_w_out, L0_attn_b_out, L0_ffn_router_w, L0_ffn_gate_w,
           L0_ffn_up_w, L0_ffn_down_w):
    import concourse.bacc as bacc
    from concourse.bass_utils import run_bass_kernel_spmd

    def laid(a, shape=None):
        a = np.ascontiguousarray(a)
        return a if shape is None else a.reshape(shape)

    arrays = dict(
        x=laid(L0_attn_x, (T, D)),
        wqkv=laid(np.asarray(L0_attn_w_qkv).T),
        wout=laid(np.asarray(L0_attn_w_out).T),
        bout=laid(L0_attn_b_out),
        router=laid(np.asarray(L0_ffn_router_w).T),
        gate=laid(np.asarray(L0_ffn_gate_w).transpose(2, 0, 1), (D, E * I)),
        up=laid(np.asarray(L0_ffn_up_w).transpose(2, 0, 1), (D, E * I)),
        down=laid(np.asarray(L0_ffn_down_w).reshape(E, D, IC, P).transpose(3, 0, 2, 1), (P, E * I)),
        const=constants(),
    )
    nc = bacc.Bacc("TRN2", target_bir_lowering=False, num_devices=1)
    args = [nc.dram_tensor(name, a.shape, F32, kind="ExternalInput").ap() for name, a in arrays.items()]
    out = nc.dram_tensor("out", (T, D), F32, kind="ExternalOutput").ap()
    moe_attention_block(nc, *args, out)
    r = run_bass_kernel_spmd(nc, [arrays], core_ids=[0])
    return r.results[0]["out"].reshape(NBATCH, SEQ, D)
```

```python
from contextlib import ExitStack

import numpy as np
import concourse.bass as bass
from concourse import mybir

F32 = mybir.dt.float32
F16 = mybir.dt.float16
I32 = mybir.dt.int32
U32 = mybir.dt.uint32
ALU = mybir.AluOpType
ACT = mybir.ActivationFunctionType
AX_X = mybir.AxisListType.X

P = 128
D = 128
NBATCH, SEQ = 4, 512
T = NBATCH * SEQ
NT = T // P
TPB = SEQ // P
H, HD = 16, 8
E, I = 8, 512
IC = I // P
TOP = 2
NS = (TOP * T + E * (P - 1)) // P
RING = 3
NR = NS // RING
AHEAD = RING + 2
assert NR * RING == NS
LN_EPS, Z_EPS = 1e-5, 1e-6
TAKEN = 1e30
NO_ROW = 2 * TOP * T

_SIZES = dict(ident=P, upper=P, ones=P, prefix=P, total=E, rev=E, tiles=NS, lanes=P, steps=NT,
              below=E * E, code=TOP * NT, heads=D, headsel=H, experts=E, powers=RING)
COL, _at = {}, 0
for _name, _n in _SIZES.items():
    COL[_name] = (_at, _at + _n)
    _at += _n
NCONST = _at
NW = D + H
POOL_TILES = 3
LOAD_ORDER = [0, NBATCH - 1, *range(1, NBATCH - 1)]
TURNED_AHEAD = 7
WARM = 5


def constants():
    c = np.zeros((P, NCONST), np.float32)
    p = np.arange(P)

    def put(name, value):
        c[:, COL[name][0]:COL[name][1]] = value

    put("ident", np.eye(P))
    put("upper", p[:, None] < p[None, :])
    put("ones", 1.0)
    tile, expert = p // E, p % E
    put("prefix", (expert[:, None] == expert) & (tile[:, None] < tile))
    put("total", expert[:, None] == np.arange(E))
    put("rev", E - np.arange(E))
    put("tiles", np.arange(NS))
    put("lanes", p)
    put("steps", P * np.arange(NT))
    put("below", (np.arange(E)[None, :] < np.arange(E)[:, None]).reshape(-1))
    token = P * np.arange(NT)[None, :] + p[:, None] + 1
    put("code", np.concatenate([-token, token], 1))
    put("heads", (p[:, None] // HD) == (p[None, :] // HD))
    put("headsel", (p[:, None] // HD) == np.arange(H))
    put("experts", np.arange(E))
    put("powers", E ** np.arange(RING))
    return c


def moe_attention_block(nc, x, wqvkr, wout, bout, gate_up, down, const, out):
    with ExitStack() as ctx:
        def sb(name, shape, dt=F32):
            return ctx.enter_context(nc.sbuf_tensor(name, shape, dt))

        def sem(name):
            return ctx.enter_context(nc.semaphore(name))

        bank = [ctx.enter_context(nc.psum_tensor(f"bank{n}", [P, 512], F32)) for n in range(8)]
        xn_rows = nc.dram_tensor("xn_rows", (T, D), F32, kind="Internal").ap()
        expert_rows = nc.dram_tensor("expert_rows", (TOP * T, D), F32, kind="Internal").ap()

        X = sb("X", [P, NT, D])
        XN = sb("XN", [P, NT, D])
        XNT = sb("XNT", [P, T])
        Wqvkr = sb("Wqvkr", [P, 3 * D + E])
        Wout = sb("Wout", [P, D])
        Bout = sb("Bout", [P, D])
        Wgu = sb("Wgu", [P, E * 2 * I])
        Wd = sb("Wd", [P, E * I])
        K = sb("K", [P, NCONST])
        stats = sb("stats", [P, NT, 6])
        mv = sb("mv", [P, NT, 2])
        var = sb("var", [P, NT])
        std = sb("std", [P, NT])
        rstd = sb("rstd", [P, NT])
        newt = sb("newt", [P, NT])
        rs = sb("rs", [P, NT])
        ek = sb("ek", [P, 2, SEQ])
        rk = sb("rk", [P, 2, SEQ])
        eq = sb("eq", [P, 2, SEQ])
        rq = sb("rq", [P, 2, SEQ])
        PK = sb("PK", [P, NBATCH, SEQ])
        PQ = sb("PQ", [P, NBATCH, SEQ])
        V1 = sb("V1", [P, NT, D + 1])
        KVD = sb("KVD", [P, NBATCH, NW])
        den = sb("den", [P, 2, 2, H])
        z = sb("z", [P, 2, 2, H])
        O = sb("O", [P, 2, TPB, D])
        OT = sb("OT", [P, 2, SEQ])
        A = sb("A", [P, NT, D])
        top = sb("top", [P, TOP, NT])
        Lg = sb("Lg", [P, NT, E])
        L2 = sb("L2", [P, NT, E])
        Ls = sb("Ls", [P, NT, E])
        Ex = sb("Ex", [P, NT, E])
        ssum = sb("ssum", [P, NT])
        rsum = sb("rsum", [P, NT])
        Pr = sb("Pr", [P, NT, E])
        cand = sb("cand", [P, NT, E])
        mark = sb("mark", [P, NT])
        OH = sb("OH", [P, TOP, NT, E])
        M16 = sb("M16", [P, NT * E], F16)
        psum2 = sb("psum2", [P, NT])
        WT = sb("WT", [P, TOP, NT, E])
        WS = sb("WS", [P, TOP, NT, E])
        WTs = sb("WTs", [P, NT, E])
        upper16 = sb("upper16", [P, P], F16)
        ones16 = sb("ones16", [P, P], F16)
        prefix16 = sb("prefix16", [P, P], F16)
        total16 = sb("total16", [P, E], F16)
        tot16 = sb("tot16", [P, P], F16)
        cnt = sb("cnt", [P, E])
        gt = sb("gt", [P, E, NT])
        ntile = sb("ntile", [P, E])
        basep = sb("basep", [P, E, E])
        base = sb("base", [P, E])
        slot = sb("slot", [P, NT, E])
        pos = sb("pos", [P, TOP, NT])
        posi = sb("posi", [P, TOP * NT], I32)
        hilo = sb("hilo", [P, 2, TOP * NT], I32)
        hilo16 = sb("hilo16", [P, 2, TOP * NT], F16)
        tiles16 = sb("tiles16", [P, NS, TOP * NT], F16)
        lanes16 = sb("lanes16", [P, P, TOP * NT], F16)
        code16 = sb("code16", [P, TOP * NT], F16)
        OHcode = sb("OHcode", [P, NS, TOP * NT], F16)
        OHlo = sb("OHlo", [P, P, TOP * NT], F16)
        code = sb("code_of_slot", [P, NS])
        row1 = sb("row1", [P, NS])
        second = sb("second", [P, NS])
        pad = sb("pad", [P, NS])
        IDX = sb("IDX", [P, NS, 2], U32)
        ge = sb("ge", [P, NS, E])
        eid = sb("eid", [P, NS])
        terms = sb("terms", [P, NR, RING])
        words = sb("words", [P, NR])
        word = sb("word", [P, NR], I32)
        sumw = sb("sumw", [P, E])
        meanw = sb("meanw", [P, E])
        scale = sb("scale", [P, NS])
        gidx = sb("gidx", [P, RING, 1], U32)
        sidx = sb("sidx", [P, RING, 1], U32)
        XG = sb("XG", [P, RING, D])
        XGT = sb("XGT", [P, RING, P])
        GU = sb("GU", [P, RING, 2, I])
        DN = sb("DN", [P, RING, I])
        SG = sb("SG", [P, RING, I])
        HG = sb("HG", [P, RING, I])
        Y = sb("Y", [P, RING, D])
        first_rows, second_rows = XN, A

        def k_(name):
            a, b = COL[name]
            return K[:, a:b]

        def over_tiles(ap, n=NT, width=E):
            return ap.unsqueeze(1).to_broadcast([P, n, width])

        def over_experts(ap, n=NT):
            return ap.unsqueeze(2).to_broadcast([P, n, E])

        x_loaded = [sem(f"x_loaded{q}") for q in range(NBATCH)]
        const_loaded = sem("const_loaded")
        attn_weights_loaded = sem("attn_weights_loaded")
        gate_up_loaded = sem("gate_up_loaded")
        down_loaded = sem("down_loaded")
        dve_step = sem("dve_step")
        newton_step = sem("newton_step")
        var_ready = sem("var_ready")
        std_ready = sem("std_ready")
        xn_ready = sem("xn_ready")
        xn_last_ready = sem("xn_last_ready")
        xn_stored = sem("xn_stored")
        xt_made = sem("xt_made")
        xt_copied = sem("xt_copied")
        consts16 = sem("consts16")
        keys_made = sem("keys_made")
        logits_taken = sem("logits_taken")
        shifted = sem("shifted")
        exp_ready = sem("exp_ready")
        chosen = sem("chosen")
        tot_made = sem("tot_made")
        tot_copied = sem("tot_copied")
        rank_made = sem("rank_made")
        weights_ready = sem("weights_ready")
        sumw_made = sem("sumw_made")
        tiles_ready = sem("tiles_ready")
        onehot_ready = sem("onehot_ready")
        code_made = sem("code_made")
        index_ready = sem("index_ready")
        word_ready = sem("word_ready")
        weight_step = sem("weight_step")
        mean_step = sem("mean_step")
        word_step = sem("word_step")
        den_ready = sem("den_ready")
        inverted = sem("inverted")
        v_made = sem("v_made")
        q_made = sem("q_made")
        k_taken = sem("k_taken")
        negative = sem("negative")
        k_terms = sem("k_terms")
        q_terms = sem("q_terms")
        v_taken = sem("v_taken")
        q_taken = sem("q_taken")
        phik_ready = sem("phik_ready")
        phiq_ready = sem("phiq_ready")
        v_ones = sem("v_ones")
        kv_made = sem("kv_made")
        kv_ready = sem("kv_ready")
        num_made = sem("num_made")
        o_ready = sem("o_ready")
        ot_made = sem("ot_made")
        ot_copied = sem("ot_copied")
        proj_made = sem("proj_made")
        proj_taken = sem("proj_taken")
        attention_added = sem("attention_added")
        bias_added = sem("bias_added")
        gathered = [sem(f"gathered{r}") for r in range(RING)]
        scattered = [sem(f"scattered{r}") for r in range(RING)]
        indices_copied = sem("indices_copied")
        xgt_made = sem("xgt_made")
        xgt_copied = sem("xgt_copied")
        gate_made = sem("gate_made")
        up_made = sem("up_made")
        silu_ready = sem("silu_ready")
        hidden_ready = sem("hidden_ready")
        gate_up_placed = sem("gate_up_placed")
        down_placed = sem("down_placed")
        y_made = sem("y_made")
        y_ready = sem("y_ready")
        first_loaded = [sem(f"first_loaded{q}") for q in range(NBATCH)]
        second_loaded = [sem(f"second_loaded{q}") for q in range(NBATCH)]
        first_added = sem("first_added")
        last_first_added = sem("last_first_added")
        last_ready = sem("last_ready")
        final_ready = sem("final_ready")
        out_stored = sem("out_stored")

        x_d = x.rearrange("(q c p) d -> q p c d", p=P, c=TPB)
        xn_d = xn_rows.rearrange("(q c p) d -> q p c d", p=P, c=TPB)
        er_d = expert_rows.rearrange("(k q c p) d -> k q p c d", k=TOP, p=P, c=TPB)
        out_d = out.rearrange("(q c p) d -> q p c d", p=P, c=TPB)

        def quarter(buf, q):
            return buf[:, q * TPB:(q + 1) * TPB, :]

        def gate_bank(r):
            return bank[(1, 6, 7)[r]]

        def up_bank(r):
            return bank[(0, 5, 2)[r]]

        def experts_of(engine, n):
            w = engine.value_load(word[0:1, n], min_val=0, max_val=E ** RING - 1)
            return [(w // E ** m) % E for m in range(RING)]

        def normalised(engine, t):
            last = NT - POOL_TILES
            engine.wait_ge(xn_ready, min(t + 1, last))
            if t >= last:
                engine.wait_ge(xn_last_ready, t + 1 - last)

        def turn_bank(q):
            return bank[4 + q]

        def keys_bank(j):
            return bank[j][:, 0:2 * (D + E)].rearrange("p (c n) -> p c n", n=D + E)

        def kv_bank(b):
            return bank[(5, 1)[b // 2]][:, b % 2 * (D + 1):(b % 2 + 1) * (D + 1)]

        def num_bank(j):
            return bank[(6, 7, 4)[j % 3]][:, 0:2 * NW].rearrange("p (c n) -> p c n", n=NW)

        def proj_bank(b):
            return bank[b % 2 * 2]

        block = ctx.enter_context(nc.Block())

        @block.sync
        def _(sp):
            for q in range(0, NBATCH, 2):
                sp.dma_start(quarter(X, q), x_d[q]).then_inc(x_loaded[q], 16)
            sp.dma_start(Wqvkr[:], wqvkr).then_inc(attn_weights_loaded, 16)
            sp.dma_start(Wout[:], wout).then_inc(attn_weights_loaded, 16)
            sp.dma_start(Bout[:], bout.partition_broadcast(P)).then_inc(attn_weights_loaded, 16)
            sp.dma_start(Wgu[:], gate_up).then_inc(gate_up_loaded, 16)
            sp.dma_start(Wd[:], down).then_inc(down_loaded, 16)
            for r in range(RING):
                sp.wait_ge(scattered[r], 16 * NR)
            for q in LOAD_ORDER:
                sp.dma_start(quarter(first_rows, q), er_d[0, q]).then_inc(first_loaded[q], 16)
            for q in range(NBATCH - 1):
                sp.wait_ge(final_ready, q + 1)
                sp.dma_start(out_d[q], quarter(X, q)).then_inc(out_stored, 16)
            sp.wait_ge(out_stored, 16 * NBATCH)

        @block.scalar
        def _(act):
            for q in range(1, NBATCH, 2):
                act.dma_start(quarter(X, q), x_d[q]).then_inc(x_loaded[q], 16)
            act.dma_start(K[:], const).then_inc(const_loaded, 16)
            for h in range(2):
                part = slice(h * NT // 2, (h + 1) * NT // 2)
                act.wait_ge(var_ready, h + 1)
                nc.scalar.activation(std[:, part], var[:, part], ACT.Sqrt).then_inc(std_ready, 1)
            nc.scalar.preload_act_table(ACT.Exp)
            for q in range(NBATCH):
                act.wait_ge(xt_made, q + 1)
                nc.scalar.copy(XNT[:, q * SEQ:(q + 1) * SEQ], turn_bank(q)[:]).then_inc(xt_copied, 1)
                normalised(act, (q + 1) * TPB - 1)
                act.dma_start(xn_d[q], quarter(XN, q)).then_inc(xn_stored, 16)
            taken = [0]

            def phi_terms(source, ez, rz):
                nc.scalar.activation(ez, source, ACT.Relu, scale=-1.0).then_inc(negative, 1)
                taken[0] += 1
                reader = nc.scalar.activation(rz, source, ACT.Relu)
                act.wait_ge(negative, taken[0])
                return reader, nc.scalar.activation(ez, ez, ACT.Exp, scale=-1.0)

            def keys(b):
                if b >= 2:
                    act.wait_ge(phik_ready, b - 1)
                for h in range(2):
                    act.wait_ge(logits_taken, 2 * b + h + 1)
                    part = slice(h * 2 * D, (h + 1) * 2 * D)
                    reader, exp = phi_terms(keys_bank(2 * b + h)[:, :, 0:D],
                                            ek[:, b % 2, part].rearrange("p (c d) -> p c d", d=D),
                                            rk[:, b % 2, part].rearrange("p (c d) -> p c d", d=D))
                reader.then_inc(k_taken, 1)
                exp.then_inc(k_terms, 1)

            def values(b):
                act.wait_ge(v_made, b + 1)
                nc.scalar.copy(V1[:, b * TPB:(b + 1) * TPB, 0:D],
                               bank[0][:].rearrange("p (c d) -> p c d", d=D)).then_inc(v_taken, 1)

            def queries(b):
                act.wait_ge(q_made, b + 1)
                if b >= 2:
                    act.wait_ge(phiq_ready, b - 1)
                reader, exp = phi_terms(bank[2][:], eq[:, b % 2], rq[:, b % 2])
                reader.then_inc(q_taken, 1)
                exp.then_inc(q_terms, 1)

            keys(0)
            act.wait_ge(shifted, 1)
            nc.scalar.activation(Ex[:], Ls[:], ACT.Exp).then_inc(exp_ready, 1)
            keys(1)
            for b in range(NBATCH):
                values(b)
                queries(b)
                if b + 2 < NBATCH:
                    keys(b + 2)
            nc.scalar.preload_act_table(ACT.Silu)

            def place_gate_up(r, e):
                nc.scalar.copy(GU[:, r].rearrange("p k i -> p (k i)"),
                               Wgu[:, bass.ds(e * (2 * I), 2 * I)]).then_inc(gate_up_placed, 1)

            def projection_taken(b):
                act.wait_ge(proj_made, b + 1)
                nc.scalar.copy(quarter(A, b), proj_bank(b)[:].rearrange("p (c d) -> p c d", d=D)).then_inc(
                    proj_taken, 1)

            for b in range(NBATCH):
                act.wait_ge(ot_made, b + 1)
                if b >= 2:
                    act.wait_ge(proj_made, b - 1)
                nc.scalar.copy(OT[:, b % 2], bank[5][:]).then_inc(ot_copied, 1)
                if b == 0:
                    projection_taken(0)
                    act.wait_ge(word_ready, 1)
                    act.wait_ge(gate_up_loaded, 16)
                    first_ids = experts_of(act, slice(0, 1))
                if 0 < b < NBATCH - 1:
                    place_gate_up(b - 1, first_ids[b - 1])
                    projection_taken(b)

            def activate(r, s, first=False):
                act.wait_ge(gate_made, s + 1)
                if not first:
                    act.wait_ge(hidden_ready, s - RING + 1)
                nc.scalar.activation(SG[:, r], gate_bank(r)[:], ACT.Silu).then_inc(silu_ready, 1)

            def turn(i, first=False, last=False):
                if not last:
                    ids = experts_of(act, slice(i + 1, i + 2) if first else bass.ds(i + 1, 1))
                for r in range(RING):
                    s = i * RING + r
                    if not last:
                        act.wait_ge(up_made, s + 1)
                        place_gate_up(r, ids[r])
                    if not last or r + 1 < RING:
                        activate((r + 1) % RING, s + 1, first and r + 1 < RING)

            activate(0, 0, first=True)
            place_gate_up(RING - 1, first_ids[RING - 1])
            projection_taken(NBATCH - 1)
            turn(0, first=True)
            with act.Fori(1, NR - 1) as i:
                turn(i)
            turn(NR - 1, last=True)

            for r in range(RING):
                act.wait_ge(scattered[r], 16 * NR)
            for q in LOAD_ORDER:
                act.dma_start(quarter(second_rows, q), er_d[1, q]).then_inc(second_loaded[q], 16)
            act.wait_ge(last_ready, 1)
            act.dma_start(out_d[NBATCH - 1], quarter(X, NBATCH - 1)).then_inc(out_stored, 16)

        @block.gpsimd
        def _(pool):
            nc.gpsimd.memset(V1[:, :, D:D + 1], 1.0).then_inc(v_ones, 1)
            pool.wait_ge(const_loaded, 16)
            nc.gpsimd.tensor_copy(upper16[:], k_("upper"))
            nc.gpsimd.tensor_copy(ones16[:], k_("ones"))
            nc.gpsimd.tensor_copy(prefix16[:], k_("prefix"))
            nc.gpsimd.tensor_copy(total16[:], k_("total")).then_inc(consts16, 1)
            pool.wait_ge(newton_step, 10)
            for t in range(NT - POOL_TILES, NT):
                nc.gpsimd.tensor_scalar(XN[:, t], X[:, t], mv[:, t, 0:1], rs[:, t:t + 1],
                                        ALU.subtract, ALU.mult).then_inc(xn_last_ready, 1)
            nc.gpsimd.tensor_copy(code16[:], k_("code"))
            nc.gpsimd.tensor_copy(tiles16[:], k_("tiles").unsqueeze(2).to_broadcast(
                [P, NS, TOP * NT])).then_inc(tiles_ready, 1)

            def phi(b):
                for terms, ez, rz, to, done in ((k_terms, ek, rk, PK, phik_ready),
                                                (q_terms, eq, rq, PQ, phiq_ready)):
                    pool.wait_ge(terms, b + 1)
                    nc.gpsimd.tensor_tensor(to[:, b], ez[:, b % 2], rz[:, b % 2], ALU.add).then_inc(done, 1)

            for b in range(NBATCH):
                phi(b)

            pool.wait_ge(index_ready, 1)
            pool.wait_ge(xn_stored, 16 * NBATCH)

            def gather(r, tile):
                nc.gpsimd.tensor_copy(gidx[:, r], IDX[:, tile, 0:1]).then_inc(indices_copied, 1)
                pool.wait_ge(indices_copied, 1)
                nc.gpsimd.indirect_dma_start(
                    XG[:, r], None, xn_rows, bass.IndirectOffsetOnAxis(gidx[:, r], 0)).then_inc(gathered[r], 16)
                pool.sem_clear(indices_copied)

            def scatter(r, tile):
                nc.gpsimd.tensor_copy(sidx[:, r], IDX[:, tile, 1:2]).then_inc(indices_copied, 1)
                pool.wait_ge(indices_copied, 1)
                nc.gpsimd.indirect_dma_start(
                    expert_rows, bass.IndirectOffsetOnAxis(sidx[:, r], 0), Y[:, r], None,
                    bounds_check=TOP * T - 1, oob_is_err=False).then_inc(scattered[r], 16)
                pool.sem_clear(indices_copied)

            def gather_next(i, r, tile):
                pool.wait_ge(xgt_made, i * RING + r + 3)
                gather((r + 2) % RING, tile)

            def scatter_made(i, r, tile):
                pool.wait_ge(y_ready, i * RING + r + 1)
                scatter(r, tile)

            for r in range(RING):
                gather(r, slice(r, r + 1))
            pool.wait_ge(attn_weights_loaded, 48)
            pool.wait_ge(xn_ready, NT - POOL_TILES)
            nc.gpsimd.tensor_tensor(X[:], X[:], Bout[:].unsqueeze(1).to_broadcast([P, NT, D]),
                                    ALU.add).then_inc(bias_added, 1)
            for r in range(AHEAD - RING):
                pool.wait_ge(xgt_made, r + 1)
                gather(r, slice(RING + r, RING + r + 1))
            with pool.Fori(0, NR - 2) as i:
                for r in range(RING):
                    gather_next(i, r, bass.ds(i * RING + r + AHEAD, 1))
                    scatter_made(i, r, bass.ds(i * RING + r, 1))
            for s in range(NS - 2 * RING, NS):
                i, r = s // RING, s % RING
                if s + AHEAD < NS:
                    gather_next(i, r, slice(s + AHEAD, s + AHEAD + 1))
                scatter_made(i, r, slice(s, s + 1))
            for r in range(RING):
                pool.wait_ge(scattered[r], 16 * NR)
            q = NBATCH - 1
            pool.wait_ge(attention_added, NBATCH)
            pool.wait_ge(first_loaded[q], 16)
            nc.gpsimd.tensor_tensor(quarter(X, q), quarter(X, q), quarter(first_rows, q),
                                    ALU.add).then_inc(last_first_added, 1)
            pool.wait_ge(last_first_added, 1)
            pool.wait_ge(second_loaded[q], 16)
            nc.gpsimd.tensor_tensor(quarter(X, q), quarter(X, q), quarter(second_rows, q),
                                    ALU.add).then_inc(last_ready, 1)

        @block.vector
        def _(dve):
            steps = [0]

            def signal(ins):
                steps[0] += 1
                ins.then_inc(dve_step, 1)

            def settle():
                dve.wait_ge(dve_step, steps[0])

            def step(ins):
                signal(ins)
                settle()

            v = nc.vector
            halves = [slice(0, NT // 2), slice(NT // 2, NT)]
            for h, part in enumerate(halves):
                for t in range(part.start, part.stop):
                    if t % TPB == 0:
                        dve.wait_ge(x_loaded[t // TPB], 16)
                    last = v.bn_stats(stats[:, t], X[:, t])
                step(last)
                for t in range(part.start, part.stop):
                    last = v.bn_aggr(mv[:, t], stats[:, t])
                step(last)
                v.tensor_scalar(var[:, part], mv[:, part, 1], LN_EPS, None, ALU.add).then_inc(var_ready, 1)

            def normalise(t):
                v.tensor_scalar(XN[:, t], X[:, t], mv[:, t, 0:1], rs[:, t:t + 1],
                                ALU.subtract, ALU.mult).then_inc(xn_ready, 1)

            for h, part in enumerate(halves):
                dve.wait_ge(std_ready, h + 1)
                v.reciprocal(rstd[:, part], std[:, part]).then_inc(newton_step, 1)
                if h:
                    normalise(0)
                dve.wait_ge(newton_step, 5 * h + 1)
                v.tensor_tensor(newt[:, part], rstd[:, part], rstd[:, part], ALU.mult).then_inc(newton_step, 1)
                if h:
                    normalise(1)
                dve.wait_ge(newton_step, 5 * h + 2)
                v.tensor_tensor(newt[:, part], newt[:, part], var[:, part], ALU.mult).then_inc(newton_step, 1)
                if h:
                    normalise(2)
                dve.wait_ge(newton_step, 5 * h + 3)
                v.tensor_scalar(newt[:, part], newt[:, part], -0.5, 1.5, ALU.mult,
                                ALU.add).then_inc(newton_step, 1)
                if h:
                    normalise(3)
                dve.wait_ge(newton_step, 5 * h + 4)
                ins = v.tensor_tensor(rs[:, part], rstd[:, part], newt[:, part], ALU.mult)
                ins.then_inc(newton_step, 1)
                if h:
                    normalise(4)
                dve.wait_ge(newton_step, 5 * h + 5)
            for t in range(5, NT - POOL_TILES):
                normalise(t)

            dve.wait_ge(const_loaded, 16)
            for j in range(NT // 2):
                if j % 2 == 0:
                    part = slice(j // 2 * (P // NBATCH), (j // 2 + 1) * (P // NBATCH))
                    v.tensor_copy(lanes16[:, part], k_("lanes")[:, part].unsqueeze(2).to_broadcast(
                        [P, P // NBATCH, TOP * NT]))
                dve.wait_ge(keys_made, j + 1)
                v.tensor_copy(Lg[:, 2 * j:2 * j + 2], keys_bank(j)[:, :, D:D + E]).then_inc(logits_taken, 1)

            L = Lg[:]
            dve.wait_ge(logits_taken, NT // 2)
            rev_of = over_tiles(k_("rev"))
            step(v.tensor_reduce(top[:, 0], L, AX_X, ALU.max))
            signal(v.tensor_tensor(cand[:], L, over_experts(top[:, 0]), ALU.is_ge))
            v.tensor_tensor(Ls[:], L, over_experts(top[:, 0]), ALU.subtract).then_inc(shifted, 1)
            settle()
            step(v.tensor_tensor(cand[:], cand[:], rev_of, ALU.mult))
            step(v.tensor_reduce(mark[:], cand[:], AX_X, ALU.max))
            step(v.tensor_tensor(OH[:, 0], rev_of, over_experts(mark[:]), ALU.is_equal))
            step(v.scalar_tensor_tensor(L2[:], OH[:, 0], -TAKEN, L, ALU.mult, ALU.add))
            step(v.tensor_reduce(top[:, 1], L2[:], AX_X, ALU.max))
            signal(v.tensor_tensor(cand[:], L2[:], over_experts(top[:, 1]), ALU.is_ge))
            dve.wait_ge(exp_ready, 1)
            v.tensor_reduce(ssum[:], Ex[:], AX_X, ALU.add)
            settle()
            step(v.tensor_tensor(cand[:], cand[:], rev_of, ALU.mult))
            signal(v.tensor_reduce(mark[:], cand[:], AX_X, ALU.max))
            v.reciprocal(rsum[:], ssum[:])
            settle()
            step(v.tensor_tensor(OH[:, 1], rev_of, over_experts(mark[:]), ALU.is_equal))
            v.tensor_tensor(M16[:].rearrange("p (t e) -> p t e", e=E), OH[:, 0], OH[:, 1],
                            ALU.add).then_inc(chosen, 1)
            step(v.tensor_tensor(Pr[:], Ex[:], over_experts(rsum[:]), ALU.mult))
            v.tensor_tensor(WT[:], OH[:], Pr[:].unsqueeze(1).to_broadcast([P, TOP, NT, E]), ALU.mult)
            dve.wait_ge(tot_made, 1)
            v.tensor_copy(tot16[:], bank[1][:, 256:384]).then_inc(tot_copied, 1)

            def kv_blocks(b):
                dve.wait_ge(kv_made, 2 * (b // 2) + 2)
                kv = kv_bank(b)
                v.tensor_tensor(KVD[:, b, 0:D], kv[:, 0:D], k_("heads"), ALU.mult)
                v.tensor_tensor(KVD[:, b, D:NW], kv[:, D:D + 1].to_broadcast([P, H]), k_("headsel"),
                                ALU.mult).then_inc(kv_ready, 1)

            dve.wait_ge(rank_made, 1)
            v.tensor_copy(cnt[:], bank[1][:, P:P + E])
            step(v.tensor_tensor(gt[:], bank[1][:, P:P + E].unsqueeze(2).to_broadcast([P, E, NT]),
                                 k_("steps").unsqueeze(1).to_broadcast([P, E, NT]), ALU.is_gt))
            step(v.tensor_reduce(ntile[:], gt[:], AX_X, ALU.add))
            step(v.tensor_tensor(basep[:], ntile[:].unsqueeze(1).to_broadcast([P, E, E]),
                                 k_("below").rearrange("p (a b) -> p a b", b=E), ALU.mult))
            step(v.tensor_reduce(base[:], basep[:], AX_X, ALU.add))
            step(v.scalar_tensor_tensor(slot[:], over_tiles(base[:]), float(P),
                                        bank[1][:, 0:P].rearrange("p (t e) -> p t e", e=E),
                                        ALU.mult, ALU.add))
            step(v.tensor_tensor(WS[:], OH[:], slot[:].unsqueeze(1).to_broadcast([P, TOP, NT, E]), ALU.mult))
            step(v.tensor_reduce(pos[:], WS[:], AX_X, ALU.add))
            step(v.tensor_copy(posi[:], pos[:].rearrange("p k t -> p (k t)")))
            v.tensor_scalar(hilo[:, 0], posi[:], 7, None, ALU.arith_shift_right)
            step(v.tensor_scalar(hilo[:, 1], posi[:], P - 1, None, ALU.bitwise_and))
            step(v.tensor_copy(hilo16[:], hilo[:]))
            dve.wait_ge(tiles_ready, 1)
            step(v.tensor_tensor(OHcode[:], tiles16[:], hilo16[:, 0:1].to_broadcast([P, NS, TOP * NT]),
                                 ALU.is_equal))
            v.tensor_tensor(OHcode[:], OHcode[:], code16[:].unsqueeze(1).to_broadcast([P, NS, TOP * NT]),
                            ALU.mult)
            kv_blocks(0)
            kv_blocks(1)
            for k in range(TOP):
                part = slice(k * NT, (k + 1) * NT)
                v.tensor_tensor(OHlo[:, :, part], lanes16[:, :, part],
                                hilo16[:, 1:2, part].to_broadcast([P, P, NT]),
                                ALU.is_equal).then_inc(onehot_ready, 1)

            def normalise_weights(j):
                if j:
                    dve.wait_ge(weight_step, j)
                if j == 0:
                    ins = v.tensor_tensor(WTs[:], WT[:, 0], WT[:, 1], ALU.add)
                elif j == 1:
                    ins = v.tensor_reduce(psum2[:], WTs[:], AX_X, ALU.add)
                elif j == 2:
                    ins = v.reciprocal(psum2[:], psum2[:])
                else:
                    v.tensor_tensor(WTs[:], WTs[:], over_experts(psum2[:]), ALU.mult).then_inc(weights_ready, 1)
                    return
                ins.then_inc(weight_step, 1)

            def mean_weight(j):
                if j:
                    dve.wait_ge(mean_step, j)
                if j == 0:
                    ins = v.tensor_scalar(cnt[:], cnt[:], 1.0, None, ALU.max)
                elif j == 1:
                    ins = v.reciprocal(cnt[:], cnt[:])
                elif j == 2:
                    ins = v.tensor_tensor(ge[:], over_tiles(k_("experts"), NS), over_experts(eid[:], NS),
                                          ALU.is_equal)
                elif j == 3:
                    dve.wait_ge(sumw_made, 1)
                    ins = v.tensor_reduce(sumw[:], bank[4][:, 0:NT * E].rearrange("p (t e) -> p e t", e=E),
                                          AX_X, ALU.add)
                elif j == 4:
                    ins = v.tensor_tensor(meanw[:], sumw[:], cnt[:], ALU.mult)
                elif j == 5:
                    ins = v.tensor_tensor(ge[:], ge[:], over_tiles(meanw[:], NS), ALU.mult)
                else:
                    ins = v.tensor_reduce(scale[:], ge[:], AX_X, ALU.add)
                ins.then_inc(mean_step, 1)

            dve.wait_ge(code_made, 1)
            step(v.tensor_copy(code[:], bank[3][:, P:P + NS]))
            step(v.scalar_tensor_tensor(row1[:], code[:], -1.0, code[:], ALU.mult, ALU.max))
            v.tensor_scalar(IDX[:, :, 0], row1[:], -1.0, 0.0, ALU.add, ALU.max)
            v.tensor_scalar(second[:], code[:], 0.0, float(T), ALU.is_gt, ALU.mult)
            step(v.tensor_scalar(pad[:], code[:], 0.0, float(NO_ROW), ALU.is_equal, ALU.mult))
            step(v.scalar_tensor_tensor(row1[:], row1[:], -1.0, second[:], ALU.add, ALU.add))
            v.tensor_tensor(IDX[:, :, 1], row1[:], pad[:], ALU.add).then_inc(index_ready, 1)

            def denominators(j):
                dve.wait_ge(num_made, j + 1)
                v.tensor_scalar(den[:, j % 2], num_bank(j)[:, :, D:NW], Z_EPS, None,
                                ALU.add).then_inc(den_ready, 1)

            def inverses(j):
                dve.wait_ge(den_ready, j + 1)
                v.reciprocal(z[:, j % 2], den[:, j % 2]).then_inc(inverted, 1)

            def divide(j):
                b, c = j // 2, j % 2 * 2
                dve.wait_ge(inverted, j + 1)
                if j >= 4:
                    dve.wait_ge(ot_made, b - 1)
                v.tensor_tensor(O[:, b % 2, c:c + 2].rearrange("p c (h d) -> p c h d", d=HD),
                                num_bank(j)[:, :, 0:D].rearrange("p c (h d) -> p c h d", d=HD),
                                z[:, j % 2].unsqueeze(3).to_broadcast([P, 2, H, HD]),
                                ALU.mult).then_inc(o_ready, 1)

            def rows_copied(n, s):
                dve.wait_ge(xgt_made, s + 1)
                v.tensor_copy(XGT[:, n], bank[3][:, 0:P]).then_inc(xgt_copied, 1)

            def word_part(j):
                if j:
                    dve.wait_ge(word_step, j)
                if j == 0:
                    ins = v.tensor_tensor(ge[:, :, 1:E], k_("tiles").unsqueeze(2).to_broadcast([P, NS, E - 1]),
                                          over_tiles(base[:, 1:E], NS, E - 1), ALU.is_ge)
                elif j == 1:
                    ins = v.tensor_reduce(eid[:], ge[:, :, 1:E], AX_X, ALU.add)
                elif j == 2:
                    ins = v.tensor_tensor(terms[:], eid[:].rearrange("p (n m) -> p n m", m=RING),
                                          k_("powers").unsqueeze(1).to_broadcast([P, NR, RING]), ALU.mult)
                elif j == 3:
                    ins = v.tensor_reduce(words[:], terms[:], AX_X, ALU.add)
                else:
                    v.tensor_copy(word[:], words[:]).then_inc(word_ready, 1)
                    return
                ins.then_inc(word_step, 1)

            word_part(0)
            denominators(0)
            for j in range(NT // 2):
                inverses(j)
                if j < 4:
                    word_part(j + 1)
                elif j == 4:
                    normalise_weights(0)
                elif j == 5:
                    normalise_weights(1)
                elif j == 6:
                    mean_weight(0)
                    normalise_weights(2)
                    mean_weight(1)
                    normalise_weights(3)
                    mean_weight(2)
                if j + 1 < NT // 2:
                    denominators(j + 1)
                divide(j)
                if j == 1:
                    kv_blocks(2)
                    kv_blocks(3)
                if j in (5, 6):
                    rows_copied(j - 5, j - 5)

            def hidden(r, s, first=False):
                dve.wait_ge(silu_ready, s + 1)
                dve.wait_ge(up_made, s + 1)
                if not first:
                    dve.wait_ge(y_made, s - RING + 1)
                v.tensor_tensor(HG[:, r], SG[:, r], up_bank(r)[:], ALU.mult).then_inc(hidden_ready, 1)

            def place_down(r, s, e, first=False):
                if not first:
                    dve.wait_ge(y_made, s - RING + 1)
                v.tensor_copy(DN[:, r], Wd[:, bass.ds(e * I, I)]).then_inc(down_placed, 1)

            def result(r, s, landed, tile):
                dve.wait_ge(y_made, s + 1)
                if landed is not None:
                    dve.wait_ge(scattered[r], landed * 16)
                v.tensor_scalar(Y[:, r], bank[4][:, 0:D], scale[:, tile], None,
                                ALU.mult).then_inc(y_ready, 1)

            def add_attention(q):
                dve.wait_ge(bias_added, 1)
                dve.wait_ge(proj_taken, q + 1)
                v.tensor_tensor(quarter(X, q), quarter(X, q), quarter(A, q),
                                ALU.add).then_inc(attention_added, 1)

            def turn(i, fixed=False, last=False):
                first = fixed and i == 0
                ids = first_ids if first else experts_of(dve, slice(i, i + 1) if fixed else bass.ds(i, 1))
                for r in range(RING):
                    s = i * RING + r
                    if not last or r + 2 < RING:
                        rows_copied((r + 2) % RING, s + 2)
                    if not first or r:
                        place_down(r, s, ids[r], first)
                    if not last or r + 1 < RING:
                        hidden((r + 1) % RING, s + 1, first and r + 1 < RING)
                    if not first or r:
                        result((r - 1) % RING, s - 1,
                               None if fixed and s - 1 < RING else i - 1 if r == 0 else i,
                               slice(s - 1, s) if fixed else bass.ds(s - 1, 1))
                    if fixed and 1 <= s <= NBATCH:
                        add_attention(s - 1)

            dve.wait_ge(word_ready, 1)
            dve.wait_ge(down_loaded, 16)
            first_ids = experts_of(dve, slice(0, 1))
            place_down(0, 0, first_ids[0], first=True)
            for j in range(3, 7):
                mean_weight(j)
            dve.wait_ge(mean_step, 7)
            hidden(0, 0, first=True)
            turn(0, fixed=True)
            turn(1, fixed=True)
            with dve.Fori(2, NR - 1) as i:
                turn(i)
            turn(NR - 1, fixed=True, last=True)
            result(RING - 1, NS - 1, NR - 1, slice(NS - 1, NS))

            def second_added(q):
                dve.wait_ge(first_added, q + 1)
                dve.wait_ge(second_loaded[q], 16)
                v.tensor_tensor(quarter(X, q), quarter(X, q), quarter(second_rows, q),
                                ALU.add).then_inc(final_ready, 1)

            dve.wait_ge(attention_added, NBATCH)
            for q in range(NBATCH - 1):
                dve.wait_ge(first_loaded[q], 16)
                v.tensor_tensor(quarter(X, q), quarter(X, q), quarter(first_rows, q),
                                ALU.add).then_inc(first_added, 1)
                second_added(q)

        @block.tensor
        def _(pe):
            mm, tp = nc.tensor.matmul, nc.tensor.transpose
            ident = k_("ident")
            pe.wait_ge(x_loaded[0], 16)
            for _ in range(WARM):
                mm(bank[7][:], X[:, 0], quarter(X, 0).rearrange("p c d -> p (c d)"), start=True, stop=True)
            pe.wait_ge(const_loaded, 16)

            def turned(t):
                normalised(pe, t)
                c = t % TPB
                ins = tp(turn_bank(t // TPB)[:, c * P:(c + 1) * P], XN[:, t], ident)
                if c == TPB - 1:
                    ins.then_inc(xt_made, 1)

            def keys(t):
                if t == 0:
                    pe.wait_ge(attn_weights_loaded, 48)
                pe.wait_ge(xt_copied, t // TPB + 1)
                ins = mm(keys_bank(t // 2)[:, t % 2], XNT[:, t * P:(t + 1) * P], Wqvkr[:, 2 * D:3 * D + E],
                         start=True, stop=True)
                if t % 2 == 1:
                    ins.then_inc(keys_made, 1)

            def values(b):
                pe.wait_ge(k_taken, 1)
                if b:
                    pe.wait_ge(v_taken, b)
                for c in range(TPB):
                    t = b * TPB + c
                    last = mm(bank[0][:, c * P:(c + 1) * P], XNT[:, t * P:(t + 1) * P], Wqvkr[:, D:2 * D],
                              start=True, stop=True)
                last.then_inc(v_made, 1)

            def queries(b):
                pe.wait_ge(k_taken, 2)
                if b:
                    pe.wait_ge(q_taken, b)
                mm(bank[2][:], Wqvkr[:, 0:D], XNT[:, b * SEQ:(b + 1) * SEQ],
                   start=True, stop=True).then_inc(q_made, 1)

            def kv_sum(b):
                pe.wait_ge(phik_ready, b + 1)
                pe.wait_ge(v_taken, b + 1)
                if b == 0:
                    pe.wait_ge(v_ones, 1)
                pe.wait_ge(k_taken, 3)
                for c in range(TPB):
                    last = mm(kv_bank(b), PK[:, b, c * P:(c + 1) * P], V1[:, b * TPB + c],
                              start=(c == 0), stop=(c == TPB - 1))
                last.then_inc(kv_made, 1)

            for t in range(NT):
                turned(t)
                if t >= TURNED_AHEAD:
                    keys(t - TURNED_AHEAD)
            for t in range(NT - TURNED_AHEAD, NT):
                keys(t)
            values(0)
            queries(0)
            pe.wait_ge(chosen, 1)
            pe.wait_ge(consts16, 1)
            mm(bank[1][:, 256:384], M16[:], ones16[:], start=True, stop=True).then_inc(tot_made, 1)
            values(1)
            pe.wait_ge(tot_copied, 1)
            mm(bank[1][:, 0:P], upper16[:], M16[:], start=True, stop=False)
            mm(bank[1][:, 0:P], tot16[:], prefix16[:], start=False, stop=True)
            mm(bank[1][:, P:P + E], tot16[:], total16[:], start=True, stop=True).then_inc(rank_made, 1)
            queries(1)
            kv_sum(0)
            values(2)
            kv_sum(1)
            queries(2)

            def numerators(j):
                pe.wait_ge(kv_ready, j // 2 + 1)
                pe.wait_ge(phiq_ready, j // 2 + 1)
                if j == 0:
                    pe.wait_ge(k_taken, NBATCH)
                if j >= 3:
                    pe.wait_ge(o_ready, j - 2)
                for c in range(2):
                    t = 2 * j + c
                    b = t // TPB
                    last = mm(num_bank(j)[:, c], PQ[:, b, (t % TPB) * P:(t % TPB + 1) * P], KVD[:, b],
                              start=True, stop=True)
                last.then_inc(num_made, 1)

            def slot_codes(k):
                pe.wait_ge(onehot_ready, k + 1)
                for c in range(k * NT, (k + 1) * NT):
                    last = mm(bank[3][:, P:P + NS], OHlo[:, :, c], OHcode[:, :, c],
                              start=(c == 0), stop=(c == TOP * NT - 1))
                if k == TOP - 1:
                    last.then_inc(code_made, 1)

            numerators(0)
            numerators(1)
            values(3)
            slot_codes(0)
            slot_codes(1)
            queries(3)
            numerators(2)
            kv_sum(2)

            def turn_out(b):
                pe.wait_ge(o_ready, 2 * b + 2)
                if b:
                    pe.wait_ge(ot_copied, b)
                for c in range(TPB):
                    last = tp(bank[5][:, c * P:(c + 1) * P], O[:, b % 2, c], ident)
                last.then_inc(ot_made, 1)

            def project_out(b):
                pe.wait_ge(ot_copied, b + 1)
                if b == 1:
                    pe.wait_ge(q_taken, NBATCH)
                if b >= 2:
                    pe.wait_ge(proj_taken, b - 1)
                for c in range(TPB):
                    last = mm(proj_bank(b)[:, c * P:(c + 1) * P], OT[:, b % 2, c * P:(c + 1) * P],
                              Wout[:], start=True, stop=True)
                last.then_inc(proj_made, 1)

            def rows_turned(r, s, turn, first=False):
                pe.wait_ge(gathered[r], turn * 16 + 16)
                if not first:
                    pe.wait_ge(xgt_copied, s)
                tp(bank[3][:, 0:P], XG[:, r], ident).then_inc(xgt_made, 1)

            def gate(r, s, first=False):
                pe.wait_ge(xgt_copied, s + 1)
                pe.wait_ge(gate_up_placed, s + 1)
                if not first:
                    pe.wait_ge(silu_ready, s - RING + 1)
                for c in range(IC):
                    last = mm(gate_bank(r)[:, c * P:(c + 1) * P], GU[:, r, 0, c * P:(c + 1) * P], XGT[:, r],
                              start=True, stop=True)
                last.then_inc(gate_made, 1)

            def up(r, s, first=False):
                if not first:
                    pe.wait_ge(hidden_ready, s - RING + 1)
                for c in range(IC):
                    last = mm(up_bank(r)[:, c * P:(c + 1) * P], GU[:, r, 1, c * P:(c + 1) * P], XGT[:, r],
                              start=True, stop=True)
                last.then_inc(up_made, 1)

            def lower(r, s, first=False):
                pe.wait_ge(hidden_ready, s + 1)
                pe.wait_ge(down_placed, s + 1)
                if first:
                    pe.wait_ge(mean_step, 4)
                else:
                    pe.wait_ge(y_ready, s)
                for c in range(IC):
                    last = mm(bank[4][:, 0:D], HG[:, r, c * P:(c + 1) * P], DN[:, r, c * D:(c + 1) * D],
                              start=(c == 0), stop=(c == IC - 1))
                last.then_inc(y_made, 1)

            kv_sum(3)
            for b in range(NBATCH):
                if 2 * b + 3 < NT // 2:
                    numerators(2 * b + 3)
                turn_out(b)
                if 2 * b + 4 < NT // 2:
                    numerators(2 * b + 4)
                if b == 1:
                    rows_turned(0, 0, 0, first=True)
                if b == 2:
                    rows_turned(1, 1, 0)
                    pe.wait_ge(weights_ready, 1)
                    mm(bank[4][:, 0:NT * E], k_("ones"), WTs[:].rearrange("p t e -> p (t e)"),
                       start=True, stop=True).then_inc(sumw_made, 1)
                if b == NBATCH - 1:
                    pe.wait_ge(proj_taken, NBATCH - 1)
                    up(0, 0, first=True)
                project_out(b)
                if b == NBATCH - 2:
                    gate(0, 0, first=True)

            def turn(i, first=False, last=False):
                for r in range(RING):
                    s = i * RING + r
                    ahead = (r + 1) % RING
                    more = not last or r + 1 < RING
                    if more:
                        gate(ahead, s + 1, first and r + 1 < RING)
                    if not last or r + 2 < RING:
                        rows_turned((r + 2) % RING, s + 2, i + (r + 2) // RING)
                    if more:
                        if first and r + 2 == RING:
                            pe.wait_ge(proj_taken, NBATCH)
                        up(ahead, s + 1, first and r + 1 < RING)
                    if not first or r:
                        lower((r - 1) % RING, s - 1, first and r == 1)

            turn(0, first=True)
            with pe.Fori(1, NR - 1) as i:
                turn(i)
            turn(NR - 1, last=True)
            lower(RING - 1, NS - 1)


def kernel(L0_attn_x, L0_attn_w_qkv, L0_attn_w_out, L0_attn_b_out, L0_ffn_router_w, L0_ffn_gate_w,
           L0_ffn_up_w, L0_ffn_down_w):
    import concourse.bacc as bacc
    from concourse.bass_utils import run_bass_kernel_spmd

    def laid(a, shape=None):
        a = np.ascontiguousarray(a)
        return a if shape is None else a.reshape(shape)

    w_q, w_k, w_v = np.split(np.asarray(L0_attn_w_qkv), 3)
    arrays = dict(
        x=laid(L0_attn_x, (T, D)),
        wqvkr=laid(np.concatenate([w_q, w_v, w_k, np.asarray(L0_ffn_router_w)]).T),
        wout=laid(np.asarray(L0_attn_w_out).T),
        bout=laid(L0_attn_b_out),
        gate_up=laid(np.stack([L0_ffn_gate_w, L0_ffn_up_w]).transpose(3, 1, 0, 2), (D, E * 2 * I)),
        down=laid(np.asarray(L0_ffn_down_w).reshape(E, D, IC, P).transpose(3, 0, 2, 1), (P, E * I)),
        const=constants(),
    )
    nc = bacc.Bacc("TRN2", target_bir_lowering=False, num_devices=1)
    args = [nc.dram_tensor(name, a.shape, F32, kind="ExternalInput").ap() for name, a in arrays.items()]
    out = nc.dram_tensor("out", (T, D), F32, kind="ExternalOutput").ap()
    moe_attention_block(nc, *args, out)
    r = run_bass_kernel_spmd(nc, [arrays], core_ids=[0])
    return r.results[0]["out"].reshape(NBATCH, SEQ, D)
```
